# Optimizing a Trainium2 kernel written in Bass

```python
import numpy as np
import jax
import jax.numpy as jnp

def _softmax(x, axis=-1):
    return jax.nn.softmax(x, axis=axis)

def _gelu(x):
    return jax.nn.gelu(x, approximate=True)

def _silu(x):
    return jax.nn.silu(x)

def _sigmoid(x):
    return jax.nn.sigmoid(x)

def _layernorm(x, axis=-1, eps=1e-05):
    m = jnp.mean(x, axis=axis, keepdims=True)
    v = jnp.var(x, axis=axis, keepdims=True)
    return (x - m) / jnp.sqrt(v + eps)

def _scatter_add(tgt, idx, src, axis=0):
    return tgt.at[idx].add(src)

def _segment_sum(src, seg, n):
    return jax.ops.segment_sum(src, seg, n)
kernel_name = 'mk_adaln_d1_jaxref_r8_2129ae'

def setup_inputs(seed: int=0):
    np.random.seed(seed)
    _w = jnp.asarray

    def _L0_attn_setup():
        import jax, jax.numpy as jnp
        import numpy as np
        key = jax.random.key(seed)
        ks = jax.random.split(key, 8)
        B, L, D, N, K = (4, 512, 128, 64, 4)
        return {'x': jax.random.normal(ks[0], (B, L, D), dtype=jnp.float32), 'conv_w': jax.random.normal(ks[1], (K, 1, D), dtype=jnp.float32) * 0.1, 'conv_b': jnp.zeros((D,), dtype=jnp.float32), 'Wp': jax.random.normal(ks[2], (D, 2 * N), dtype=jnp.float32) * (1.0 / np.sqrt(D)), 'bp': jnp.zeros((2 * N,), dtype=jnp.float32), 'Ws': jax.random.normal(ks[3], (D, N), dtype=jnp.float32) * (1.0 / np.sqrt(D)), 'bs': jnp.zeros((N,), dtype=jnp.float32), 'A_log': jax.random.normal(ks[4], (N,), dtype=jnp.float32) * 0.02, 'dt_log': jax.random.normal(ks[5], (N,), dtype=jnp.float32) * 0.02, 'Wo': jax.random.normal(ks[6], (N, D), dtype=jnp.float32) * (1.0 / np.sqrt(N)), 'bo': jnp.zeros((D,), dtype=jnp.float32)}
    _L0_attn_in = _L0_attn_setup()

    def _L0_ffn_setup():
        import jax, jax.numpy as jnp
        import numpy as np
        B, L, D = (1, 256, 128)
        E, H, G, K = (64, 32, 64, 16)

        def _grouped_routing_scores(router_scores):
            T, En = router_scores.shape
            Tq = T // G
            budget = Tq * K
            order = jnp.argsort(-router_scores, axis=0)
            sorted_vals = jnp.take_along_axis(router_scores, order, axis=0)
            group_score = sorted_vals.reshape(Tq, G, En).sum(axis=1)
            _, top_flat = jax.lax.top_k(group_score.reshape(-1), budget)
            gmask = jnp.zeros((Tq * En,), bool).at[top_flat].set(True).reshape(Tq, En)
            mask_sorted = jnp.broadcast_to(gmask[:, None, :], (Tq, G, En)).reshape(T, En)
            mask = jnp.zeros((T, En), bool).at[order, jnp.arange(En)[None, :]].set(mask_sorted)
            fs = jnp.where(mask, router_scores, 0.0)
            return fs / (fs.sum(axis=-1, keepdims=True) + 1e-06)
        key = jax.random.key(seed)
        ks = jax.random.split(key, 6)
        s = lambda k, shape, scale: jax.random.normal(k, shape, jnp.float32) * scale
        return {'x': jax.random.normal(ks[0], (B, L, D), jnp.float32), 'Wr': s(ks[1], (D, E), D ** (-0.5)), 'br': jnp.zeros((E,), jnp.float32), 'Wup': s(ks[2], (E, D, H), D ** (-0.5)), 'bup': jnp.zeros((E, H), jnp.float32), 'Wgate': s(ks[3], (E, D, H), D ** (-0.5)), 'bgate': jnp.zeros((E, H), jnp.float32), 'Wdown': s(ks[4], (E, H, D), H ** (-0.5)), 'bdown': jnp.zeros((E, D), jnp.float32)}
    _L0_ffn_in = _L0_ffn_setup()
    _L0_c = _w((lambda *s: np.random.randn(*s).astype(np.float32) * 0.05)(32, 128))
    _L0_wmod = _w((lambda *s: np.random.randn(*s).astype(np.float32) * 0.05)(128, 6 * 128) * 128 ** (-0.5))
    _d = {'L0_attn_x': _L0_attn_in['x'], 'L0_attn_conv_w': _L0_attn_in['conv_w'], 'L0_attn_conv_b': _L0_attn_in['conv_b'], 'L0_attn_Wp': _L0_attn_in['Wp'], 'L0_attn_bp': _L0_attn_in['bp'], 'L0_attn_Ws': _L0_attn_in['Ws'], 'L0_attn_bs': _L0_attn_in['bs'], 'L0_attn_A_log': _L0_attn_in['A_log'], 'L0_attn_dt_log': _L0_attn_in['dt_log'], 'L0_attn_Wo': _L0_attn_in['Wo'], 'L0_attn_bo': _L0_attn_in['bo'], 'L0_ffn_Wr': _L0_ffn_in['Wr'], 'L0_ffn_br': _L0_ffn_in['br'], 'L0_ffn_Wup': _L0_ffn_in['Wup'], 'L0_ffn_bup': _L0_ffn_in['bup'], 'L0_ffn_Wgate': _L0_ffn_in['Wgate'], 'L0_ffn_bgate': _L0_ffn_in['bgate'], 'L0_ffn_Wdown': _L0_ffn_in['Wdown'], 'L0_ffn_bdown': _L0_ffn_in['bdown'], 'L0_c': _L0_c, 'L0_wmod': _L0_wmod}
    _x0 = _d['L0_attn_x']
    _d['L0_attn_x'] = jax.random.normal(jax.random.fold_in(jax.random.key(seed), 1), (32, 256, 128), dtype=_x0.dtype)
    del _x0
    return _d

def reference(L0_attn_x, L0_attn_conv_w, L0_attn_conv_b, L0_attn_Wp, L0_attn_bp, L0_attn_Ws, L0_attn_bs, L0_attn_A_log, L0_attn_dt_log, L0_attn_Wo, L0_attn_bo, L0_ffn_Wr, L0_ffn_br, L0_ffn_Wup, L0_ffn_bup, L0_ffn_Wgate, L0_ffn_bgate, L0_ffn_Wdown, L0_ffn_bdown, L0_c, L0_wmod):

    def _L0_attn_ref(x, conv_w, conv_b, Wp, bp, Ws, bs, A_log, dt_log, Wo, bo):
        import jax, jax.numpy as jnp
        import numpy as np
        B, L, D = x.shape
        K = conv_w.shape[0]
        N = Ws.shape[1]
        x_pad = jnp.pad(x, ((0, 0), (K - 1, 0), (0, 0)))
        conv = conv_b + sum((x_pad[:, k:k + L, :] * conv_w[k, 0] for k in range(K)))
        proj = conv @ Wp + bp
        B_t = jax.nn.softplus(proj[..., :N])
        C_t = jnp.tanh(proj[..., N:])
        u = x @ Ws + bs
        A = -jax.nn.softplus(A_log)
        dt = jax.nn.softplus(dt_log)
        decay = 1.0 + dt * A

        def step(state, inputs):
            u_t, b_t, c_t = inputs
            state = decay * state + dt * b_t * u_t
            return (state, c_t * state)
        init = jnp.zeros((B, N), dtype=x.dtype)
        xs = tuple((jnp.swapaxes(a, 0, 1) for a in (u, B_t, C_t)))
        _, ys = jax.lax.scan(step, init, xs, unroll=4)
        y = jnp.swapaxes(ys, 0, 1)
        return y @ Wo + bo

    def _L0_ffn_ref(x, Wr, br, Wup, bup, Wgate, bgate, Wdown, bdown):
        import jax, jax.numpy as jnp
        import numpy as np
        B, L, D = (1, 256, 128)
        E, H, G, K = (64, 32, 64, 16)

        def _grouped_routing_scores(router_scores):
            T, En = router_scores.shape
            Tq = T // G
            budget = Tq * K
            order = jnp.argsort(-router_scores, axis=0)
            sorted_vals = jnp.take_along_axis(router_scores, order, axis=0)
            group_score = sorted_vals.reshape(Tq, G, En).sum(axis=1)
            _, top_flat = jax.lax.top_k(group_score.reshape(-1), budget)
            gmask = jnp.zeros((Tq * En,), bool).at[top_flat].set(True).reshape(Tq, En)
            mask_sorted = jnp.broadcast_to(gmask[:, None, :], (Tq, G, En)).reshape(T, En)
            mask = jnp.zeros((T, En), bool).at[order, jnp.arange(En)[None, :]].set(mask_sorted)
            fs = jnp.where(mask, router_scores, 0.0)
            return fs / (fs.sum(axis=-1, keepdims=True) + 1e-06)
        Bx, Lx, Dx = x.shape
        xt = x.reshape(-1, Dx)
        router_scores = jax.nn.softmax(xt @ Wr + br, axis=-1)
        fs = _grouped_routing_scores(router_scores)
        up = jnp.einsum('td,edh->teh', xt, Wup) + bup
        gate = jnp.einsum('td,edh->teh', xt, Wgate) + bgate
        h = jax.nn.silu(up) * gate * fs[:, :, None]
        out = jnp.einsum('teh,ehd->td', h, Wdown) + fs @ bdown
        return out.reshape(Bx, Lx, Dx)
    x = L0_attn_x
    mod = (_silu(L0_c) @ L0_wmod).reshape(L0_c.shape[0], 6, 1, -1)
    sa, ca, ga, sb, cb, gb = (mod[:, 0], mod[:, 1], mod[:, 2], mod[:, 3], mod[:, 4], mod[:, 5])
    ga = (2 * (ga >= 0) - 1) * jnp.maximum(jnp.abs(ga), 0.25)
    gb = (2 * (gb >= 0) - 1) * jnp.maximum(jnp.abs(gb), 0.25)
    h = _layernorm(x, axis=-1) * (1 + ca) + sa
    x = x + ga * _L0_attn_ref(h, L0_attn_conv_w, L0_attn_conv_b, L0_attn_Wp, L0_attn_bp, L0_attn_Ws, L0_attn_bs, L0_attn_A_log, L0_attn_dt_log, L0_attn_Wo, L0_attn_bo)
    h = _layernorm(x, axis=-1) * (1 + cb) + sb
    x = x + gb * _L0_ffn_ref(h, L0_ffn_Wr, L0_ffn_br, L0_ffn_Wup, L0_ffn_bup, L0_ffn_Wgate, L0_ffn_bgate, L0_ffn_Wdown, L0_ffn_bdown)
    return x

_drawn_inputs = setup_inputs


def setup_inputs(seed=0):
    import zlib

    import numpy as np

    out = dict(_drawn_inputs(seed))
    spreads = {'L0_attn_conv_b': (0.0, 0.447),
     'L0_attn_bp': (0.0, 0.547),
     'L0_attn_bs': (0.0, 0.8),
     'L0_attn_bo': (0.0, 0.321),
     'L0_ffn_br': (0.0, 0.8),
     'L0_ffn_bup': (0.0, 0.8),
     'L0_ffn_bgate': (0.0, 0.8),
     'L0_ffn_bdown': (0.0, 0.8)}
    factors = {'L0_attn_A_log': 26.768, 'L0_attn_dt_log': 37.275}
    for name, (base, spread) in spreads.items():
        noise = np.random.default_rng([zlib.crc32(name.encode()), seed]).standard_normal(out[name].shape)
        drawn = base * np.exp(spread * noise) if base else spread * noise
        out[name] = jnp.asarray(drawn.astype(out[name].dtype))
    for name, factor in factors.items():
        out[name] = (out[name] * factor).astype(out[name].dtype)
    return out
```

```python
from contextlib import ExitStack

import concourse.bass as bass
from concourse import mybir

F32 = mybir.dt.float32
F16 = mybir.dt.float16
I32 = mybir.dt.int32
ALU = mybir.AluOpType
ACT = mybir.ActivationFunctionType
AX = mybir.AxisListType

P = 128
CONSTS = ["ident", "ones", "same_half", "before", "from_half0", "shift_up", "pair_sum", "rank"]
CLAMP = 30.0
W_SCALE = 32.0
FS_SCALE = 4096.0


class Chain:

    def __init__(self, eng, sem, start=0):
        self.eng, self.sem, self.n = eng, sem, start

    def add(self, ins):
        ins.then_inc(self.sem, 1)
        self.n = self.n + 1

    def then_wait(self, ins):
        self.add(ins)
        self.eng.wait_ge(self.sem, self.n)


def wait_pairs(eng, sem, n):
    if not isinstance(n, int) or n > 0:
        eng.wait_ge(sem, n)


def adaln_kernel(nc, x, Wp, Ws, Wo, Wr, br, Wup, Wgate, Wdown, bdown, c, wmod, params, consts, sel_const, out):
    B, L, D = x.shape
    N = Ws.shape[1]
    E = Wr.shape[1]
    H = Wup.shape[1] // E
    TAPS = params.shape[1] - 6 - 2 * (E * H // P)
    PAIRS = B // 2
    PT = 2 * L
    TILES = PT // P
    HALF = PAIRS * L
    CH = E * H // P
    EC = P // H
    G = 64
    BUDGET = (B * L // G) * 16
    NG = HALF // G
    EPS = 1e-5
    PAD = TAPS - 1
    ROW = L + PAD

    with ExitStack() as ctx:
        def sb(name, shape, dt=F32):
            return ctx.enter_context(nc.sbuf_tensor(name, shape, dt))

        def sem(name):
            return ctx.enter_context(nc.semaphore(name))

        bank = [ctx.enter_context(nc.psum_tensor(f"bank{k}", [P, 512], F32)) for k in range(8)]

        xres = sb("xres", [P, PAIRS * PT])
        scores = sb("scores", [P, HALF])
        h2_hi = sb("h2_hi", [P, PAIRS * PT], F16)
        h2_lo = sb("h2_lo", [P, PAIRS * PT], F16)
        cst = sb("cst", [P, 7 * P + NG + 4])
        sel = sb("sel", [P, CH * P], F16)
        up_hi, up_lo = sb("up_hi", [P, CH * P], F16), sb("up_lo", [P, CH * P], F16)
        gate_hi, gate_lo = sb("gate_hi", [P, CH * P], F16), sb("gate_lo", [P, CH * P], F16)
        down_hi, down_lo = sb("down_hi", [P, CH * P], F16), sb("down_lo", [P, CH * P], F16)
        mod = sb("mod", [P, 6, B])
        ga_bo = sb("ga_bo", [P, B])
        sort_a, sort_b, sort_c = sb("sort_a", [P, HALF]), sb("sort_b", [P, HALF]), sb("sort_c", [P, HALF])
        wtap = sb("wtap", [P, TAPS, 2 * N])
        wp_sb, ws_sb = sb("wp_sb", [P, 2 * N]), sb("ws_sb", [P, N])
        wo_a, wo_b = sb("wo_a", [P, D]), sb("wo_b", [P, D])
        wr_sb = sb("wr_sb", [P, E])
        bd_a, bd_b = sb("bd_a", [P, D]), sb("bd_b", [P, D])
        br_row = sb("br_row", [P, E])
        par = sb("par", [P, TAPS + 6 + 2 * CH])
        conv_sb, cols = par[:, 0:TAPS], par[:, TAPS:TAPS + 3]
        ssm_in = par[:, TAPS + 3:TAPS + 6]
        bup_c, bgate_c = par[:, TAPS + 6:TAPS + 6 + CH], par[:, TAPS + 6 + CH:TAPS + 6 + 2 * CH]
        ssm = sb("ssm", [P, 24])
        c_sb, cs_sb, cT = sb("c_sb", [B, D]), sb("cs_sb", [B, D]), sb("cT", [P, B])
        tmp6 = sb("tmp6", [P, 3, 2 * B])
        bias_p = sb("bias_p", [P, 2])
        decay_row = sb("decay_row", [P, L])
        tick = sb("tick", [P, 2])
        stat, mv = sb("stat", [P, 2, TILES, 6]), sb("mv", [P, 2, TILES, 2])
        rstd = sb("rstd", [P, 2, 5, TILES])
        s1_buf = [sort_c[:, 6 * D + k * PT:6 * D + (k + 1) * PT] for k in range(6)]
        xn1, xn2 = (v.rearrange("p (t d) -> p t d", d=D) for v in s1_buf[0:2])
        hT = sb("hT", [P, 2, ROW])
        tcl, ex1, ln_c = s1_buf[2:5]
        sp, over, ub, qd = sb("sp", [P, L]), sb("over", [P, L]), sb("ub", [P, L]), sb("qd", [P, L])
        cd, spo, bu, state, y = sb("cd", [P, L]), sb("spo", [P, L]), sb("bu", [P, L]), sb("state", [P, L]), sb("y", [P, L])
        att, h2 = s1_buf[5], sb("h2", [P, PT])
        lg, lgm, exl, sc = (sb(n, [P, TILES, E]) for n in ("lg", "lgm", "exl", "sc"))
        smx = sb("smx", [P, 3, TILES])
        gsum, gmin, gw = sb("gsum", [P, NG]), sb("gmin", [P, NG]), sb("gw", [P, 6, NG])
        bits = sb("bits", [P, 6], I32)
        rc = sb("rc", [P, 24])
        sl, g1, act = (sort_a[:, k * 2 * PT:(k + 1) * 2 * PT].rearrange("p (r t) -> p r t", r=2) for k in range(3))
        act_hi, act_lo = (sort_b[:, k * 2 * PT:(k + 1) * 2 * PT].bitcast(F16).rearrange("p (r t) -> p r t", r=4)
                          for k in range(2))
        fs2 = sb("fs2", [P, 2 * PT], F16)
        fsn, den = sb("fsn", [P, L]), sb("den", [P, 2, L])
        fs_h1 = sb("fs_h1", [P, L], F16)
        oT = sort_b[:, 4 * PT:5 * PT]

        def const(name):
            k = CONSTS.index(name)
            return cst[:, k * P:(k + 1) * P] if name != "rank" else cst[:, k * P:k * P + NG]
        eps_c = cst[:, 7 * P + NG:7 * P + NG + 1]
        one_c = cst[:, 7 * P + NG + 1:7 * P + NG + 2]
        topbit_c = cst[:, 7 * P + NG + 2:7 * P + NG + 3]
        expscale_c = cst[:, 7 * P + NG + 3:7 * P + NG + 4]
        ident = const("ident")

        params_in, w_in, br_in, x_in, x_half = (sem(n) for n in ("params_in", "w_in", "br_in", "x_in", "x_half"))
        c_silu, cT_done, cT_copied, mod_done = (sem(n) for n in ("c_silu", "cT_done", "cT_copied", "mod_done"))
        biasp_done, setup_step, prep_done, ssm_step, ssm_done = (
            sem(n) for n in ("biasp_done", "setup_step", "prep_done", "ssm_step", "ssm_done"))
        zeroed, wsplit_step, wsplit_done = sem("zeroed"), sem("wsplit_step"), sem("wsplit_done")
        mv_ready, rs_step, rs_ready = ([sem(f"{n}{k}") for k in (1, 2)] for n in ("mv_ready", "rs_step", "rs_ready"))
        stat_step, norm_step, xn_ready = ([sem(f"{n}{k}") for k in (1, 2)] for n in ("stat_step", "norm_step", "xn_ready"))
        tr1_done, h_ready, proj_done, clamped, gate_step, gates_ready = (
            sem(n) for n in ("tr1_done", "h_ready", "proj_done", "clamped", "gate_step", "gates_ready"))
        scan_step, y_ready, wo_done, att_ready, tr2_done, resid_done = (
            sem(n) for n in ("scan_step", "y_ready", "wo_done", "att_ready", "tr2_done", "resid_done"))
        tr3_done, h2_ready, split_step, split_done, router_done = (
            sem(n) for n in ("tr3_done", "h2_ready", "split_step", "split_done", "router_done"))
        sm_step, shifted, exp_done, norm_done, sc_ready, tr4_done, s_ready = (
            sem(n) for n in ("sm_step", "shifted", "exp_done", "norm_done", "sc_ready", "tr4_done", "s_ready"))
        sort_step, swap_in, route_step, cnt_ready, cnt_summed = (
            sem(n) for n in ("sort_step", "swap_in", "route_step", "cnt_ready", "cnt_summed"))
        tie_ready, tie_done, rsum_ready, rsum_done, vswap_ready, vswap_in, fs_ready = (
            sem(n) for n in ("tie_ready", "tie_done", "rsum_ready", "rsum_done", "vswap_ready", "vswap_in", "fs_ready"))
        den_done, den_step, fsn_ready, fs_hi_ready, fs2_ready = (
            sem(n) for n in ("den_done", "den_step", "fsn_ready", "fs_hi_ready", "fs2_ready"))
        up_done, gate_done, fsb_done, silu_done, gated, weighted, hi_ready, lo_ready, down_done = (
            sem(n) for n in ("up_done", "gate_done", "fsb_done", "silu_done", "gated", "weighted", "hi_ready",
                             "lo_ready", "down_done"))
        out_done, o_ready, tr5_done, fin_ready, stored = (
            sem(n) for n in ("out_done", "o_ready", "tr5_done", "fin_ready", "stored"))

        x_view = x.rearrange("(h j) (s p) d -> j h p s d", h=2, p=P)
        out_view = out.rearrange("(h j) (s p) d -> j h p s d", h=2, p=P)

        def pair_cols(t, i, w=PT):
            return t[:, bass.ds(i * w, w)]

        N_PARAMS = 16 * 13
        N_WEIGHTS = 3

        bufs = [sort_a, sort_b]

        def flip(t, k):
            v = t[:].rearrange("p (n k) -> p n k", k=k)
            return v[:, :, 0:k // 2], v[:, :, k - 1:k // 2 - 1:-1] if k > 2 else v[:, :, 1:2]

        def apart(t, j):
            v = t[:].rearrange("p (n a j) -> p n a j", a=2, j=j)
            return v[:, :, 0, :], v[:, :, 1, :]

        plan = []
        k = 2
        while k <= HALF:
            plan.append((flip, k))
            j = k // 4
            while j >= 1:
                plan.append((apart, j))
                j //= 2
            k *= 2
        MERGE = []
        j = HALF // 2
        while j >= G:
            MERGE.append((apart, j))
            j //= 2
        SORTED = 2 * len(plan)
        sorted_in = bufs[(len(plan) - 1) % 2]
        merged_in = bufs[len(plan) % 2]

        block = ctx.enter_context(nc.Block())

        @block.sync
        def _(sp_eng):
            def load(dst, src):
                sp_eng.dma_start(dst, src).then_inc(params_in, 16)

            load(cst[:], consts)
            load(c_sb[:], c)
            load(sort_c[:, 0:6 * D], wmod)
            load(wp_sb[:], Wp)
            load(ws_sb[:], Ws)
            load(wr_sb[:], Wr)
            load(par[:], params)
            load(br_row[:], br.partition_broadcast(P))
            load(sel[:], sel_const)
            load(wo_a[0:N, :], Wo)
            load(wo_b[N:P, :], Wo)
            load(bd_a[0:E, :], bdown)
            load(bd_b[E:P, :], bdown)
            def load_pair(i):
                for h in range(2):
                    sp_eng.dma_start(pair_cols(xres, i)[:, h * L:(h + 1) * L].rearrange("p (s d) -> p s d", d=D),
                                     x_view[bass.ds(i, 1), h].rearrange("a p s d -> (a p) s d")).then_inc(x_in, 16)

            load_pair(0)
            with sp_eng.Fori(1, PAIRS) as i:
                sp_eng.wait_ge(x_in, 32 * i)
                load_pair(i)
            for piece in range(2):
                cut = slice(piece * HALF // 2, (piece + 1) * HALF // 2)
                if piece == 0:
                    sp_eng.wait_ge(sort_step, SORTED)
                sp_eng.dma_start(sort_c[0:E, cut], sorted_in[E:P, cut]).then_inc(swap_in, 16)
                sp_eng.dma_start(sort_c[E:P, cut], sorted_in[0:E, cut]).then_inc(swap_in, 16)
            sp_eng.wait_ge(vswap_ready, 1)
            sp_eng.dma_start(rc[0:E, 9:10], rc[E:P, 8:9]).then_inc(vswap_in, 16)
            sp_eng.dma_start(rc[E:P, 9:10], rc[0:E, 8:9]).then_inc(vswap_in, 16)
            with sp_eng.Fori(0, PAIRS) as i:
                sp_eng.wait_ge(fin_ready, i + 1)
                for h in range(2):
                    sp_eng.dma_start(out_view[bass.ds(i, 1), h].rearrange("a p s d -> (a p) s d"),
                                     pair_cols(xres, i)[:, h * L:(h + 1) * L].rearrange("p (s d) -> p s d", d=D)
                                     ).then_inc(stored, 16)
            sp_eng.wait_ge(stored, 32 * PAIRS)

        t1_ps, proj_ps, u_ps, o_ps, t2_ps, t3_ps, lg_ps, t4_ps = bank

        @block.gpsimd
        def _(pool):
            zeros = Chain(pool, zeroed)
            for t in (wo_a[N:P, :], wo_b[0:N, :], bd_a[E:P, :], bd_b[0:E, :], hT[:]):
                zeros.then_wait(nc.gpsimd.memset(t, 0.0))
            steps = Chain(pool, wsplit_step)
            pool.wait_ge(w_in, 48)
            raw = [(sort_a[:, 0:2048], up_hi, up_lo), (sort_a[:, 2048:4096], gate_hi, gate_lo),
                   (sort_b[:, 0:2048], down_hi, down_lo)]
            for raw_k, (w, hi, lo) in enumerate(raw):
                steps.then_wait(nc.gpsimd.tensor_scalar(w, w, W_SCALE, None, ALU.mult))
                steps.then_wait(nc.gpsimd.tensor_copy(hi[:], w))
                nc.gpsimd.tensor_tensor(lo[:], w, hi[:], ALU.subtract).then_inc(wsplit_done, 1)
                pool.wait_ge(wsplit_done, raw_k + 1)
            with pool.Fori(0, PAIRS) as i:
                pool.wait_ge(h2_ready, i + 1)
                nc.gpsimd.tensor_copy(pair_cols(h2_hi, i), h2[:]).then_inc(split_step, 1)
                pool.wait_ge(split_step, i + 1)
                nc.gpsimd.tensor_tensor(pair_cols(h2_lo, i), h2[:], pair_cols(h2_hi, i),
                                        ALU.subtract).then_inc(split_done, 1)
                pool.wait_ge(split_done, i + 1)

        @block.vector
        def _(dve):
            V = nc.vector
            setup = Chain(dve, setup_step)
            dve.wait_ge(params_in, N_PARAMS)
            for k in range(TAPS):
                setup.add(V.tensor_scalar(wtap[:, k, :], wp_sb[:], conv_sb[:, k:k + 1], None, ALU.mult))
            setup.add(V.tensor_scalar(ssm[:, 4:6], ssm_in[:, 1:3], CLAMP, None, ALU.min))
            V.tensor_scalar(ssm[:, 6:8], ssm_in[:, 1:3], CLAMP, 0.0, ALU.subtract, ALU.max).then_inc(ssm_step, 1)
            dve.wait_ge(ssm_done, 2)
            dve.wait_ge(ssm_step, 1)
            setup.then_wait(V.tensor_tensor(ssm[:, 12:14], ssm[:, 6:8], ssm[:, 10:12], ALU.add))
            setup.then_wait(V.tensor_tensor(ssm[:, 14:15], ssm[:, 12:13], ssm[:, 13:14], ALU.mult))
            setup.then_wait(V.tensor_scalar(ssm[:, 15:16], ssm[:, 14:15], -1.0, 1.0, ALU.mult, ALU.add))
            setup.then_wait(V.memset(decay_row[:], 0.0))
            setup.then_wait(V.tensor_scalar(decay_row[:], decay_row[:], ssm[:, 15:16], None, ALU.add))
            setup.then_wait(V.tensor_tensor(ssm[:, 16:17], ssm_in[:, 0:1], ssm[:, 13:14], ALU.mult))
            dve.wait_ge(cT_done, 1)
            V.tensor_copy(cT[:], bank[0][:, 0:B]).then_inc(cT_copied, 1)
            dve.wait_ge(mod_done, 1)
            setup.then_wait(V.tensor_copy(mod[:], bank[1][:, 0:6 * B].rearrange("p (m b) -> p m b", b=B)))
            for m in (1, 4):
                setup.then_wait(V.tensor_scalar(mod[:, m, :], mod[:, m, :], 1.0, None, ALU.add))
            for m in (2, 5):
                setup.then_wait(V.tensor_scalar(tmp6[:, 0, 0:B], mod[:, m, :], 0.0, 2.0, ALU.is_ge, ALU.mult))
                setup.then_wait(V.tensor_scalar(tmp6[:, 1, 0:B], mod[:, m, :], -1.0, None, ALU.mult))
                setup.then_wait(V.tensor_tensor(tmp6[:, 2, 0:B], mod[:, m, :], tmp6[:, 1, 0:B], ALU.max))
                setup.then_wait(V.tensor_scalar(tmp6[:, 2, 0:B], tmp6[:, 2, 0:B], 0.25, None, ALU.max))
                setup.then_wait(V.tensor_scalar(tmp6[:, 0, 0:B], tmp6[:, 0, 0:B], 1.0, None, ALU.subtract))
                setup.then_wait(V.tensor_tensor(mod[:, m, :], tmp6[:, 2, 0:B], tmp6[:, 0, 0:B], ALU.mult))
            setup.then_wait(V.tensor_scalar(ga_bo[:], mod[:, 2, :], cols[:, 2:3], None, ALU.mult))
            setup.then_wait(V.tensor_scalar(mod[:, 5, :], mod[:, 5, :], 1.0 / W_SCALE, None, ALU.mult))
            setup.then_wait(V.tensor_scalar(bgate_c[:], bgate_c[:], W_SCALE, None, ALU.mult))
            dve.wait_ge(zeroed, 5)
            setup.then_wait(V.tensor_scalar(bd_a[:], bd_a[:], W_SCALE, None, ALU.mult))
            setup.then_wait(V.tensor_scalar(bd_b[:], bd_b[:], W_SCALE, None, ALU.mult))
            dve.wait_ge(biasp_done, 1)
            setup.then_wait(V.tensor_tensor(bias_p[:, 0:1], bank[2][:, 0:1], cols[:, 1:2], ALU.add))
            V.tensor_scalar(bias_p[:, 1:2], bias_p[:, 0:1], CLAMP, None, ALU.subtract).then_inc(prep_done, 1)

            def stats(i, which):
                v = pair_cols(xres, i).rearrange("p (t d) -> p t d", d=D)
                steps = Chain(dve, stat_step[which], i * TILES)
                V.memset(tick[:, 0:1], 0.0)
                for t in range(TILES):
                    steps.add(V.bn_stats(stat[:, which, t, :], v[:, t, :]))
                dve.wait_ge(stat_step[which], steps.n)
                V.memset(tick[:, 1:2], 0.0)
                for t in range(TILES):
                    last = V.bn_aggr(mv[:, which, t, :], stat[:, which, t, :])
                last.then_inc(mv_ready[which], 1)

            def stats1(i):
                dve.wait_ge(x_in, 32 * i + 32)
                stats(i, 0)

            def norm(i, which, xn, xn_read):
                v = pair_cols(xres, i).rearrange("p (t d) -> p t d", d=D)
                r, var = rstd[:, which], mv[:, which, :, 1]
                dve.wait_ge(rs_ready[which], i + 1)
                steps = Chain(dve, norm_step[which], i * 4)
                steps.then_wait(V.tensor_tensor(r[:, 2, :], r[:, 1, :], r[:, 1, :], ALU.mult))
                steps.then_wait(V.scalar_tensor_tensor(r[:, 3, :], var, EPS, r[:, 2, :], ALU.add, ALU.mult))
                steps.then_wait(V.tensor_scalar(r[:, 2, :], r[:, 3, :], -0.5, 1.5, ALU.mult, ALU.add))
                steps.then_wait(V.tensor_tensor(r[:, 4, :], r[:, 1, :], r[:, 2, :], ALU.mult))
                wait_pairs(dve, xn_read, i)
                for t in range(TILES):
                    last = V.tensor_scalar(xn[:, t, :], v[:, t, :], mv[:, which, t, 0:1], r[:, 4, t:t + 1],
                                           ALU.subtract, ALU.mult)
                last.then_inc(xn_ready[which], 1)

            def clamp(i):
                dve.wait_ge(proj_done, i + 1)
                V.tensor_scalar(tcl[:], proj_ps[:], bias_p[:, 0:1], CLAMP, ALU.add, ALU.min).then_inc(clamped, 1)

            def scan(i):
                dve.wait_ge(gates_ready, i + 1)
                steps = Chain(dve, scan_step, i * 4)
                steps.add(V.tensor_scalar(cd[:], qd[:], -2.0, 1.0, ALU.mult, ALU.add))
                steps.then_wait(V.tensor_tensor(spo[:], sp[:], over[:], ALU.add))
                steps.then_wait(V.tensor_tensor(bu[:], spo[:], ub[:], ALU.mult))
                steps.then_wait(V.tensor_tensor_scan(state[:], decay_row[:], bu[:], 0.0, ALU.mult, ALU.add))
                wait_pairs(dve, wo_done, i)
                V.tensor_tensor(y[:], cd[:], state[:], ALU.mult).then_inc(y_ready, 1)

            def residual(i):
                dve.wait_ge(tr2_done, i + 1)
                V.tensor_tensor(pair_cols(xres, i), t2_ps[:], pair_cols(xres, i), ALU.add).then_inc(resid_done, 1)
                dve.wait_ge(resid_done, i + 1)
                stats(i, 1)

            def softmax_shift(i):
                dve.wait_ge(router_done, i + 1)
                steps = Chain(dve, sm_step, i * 4)
                steps.then_wait(V.tensor_tensor(lg[:], lg_ps[:, 0:TILES * E].rearrange("p (t e) -> p t e", e=E),
                                                br_row[:].unsqueeze(1).to_broadcast([P, TILES, E]), ALU.add))
                steps.then_wait(V.tensor_reduce(smx[:, 0, :], lg[:], AX.X, ALU.max))
                V.tensor_tensor(lgm[:], lg[:], smx[:, 0, :].unsqueeze(2).to_broadcast([P, TILES, E]),
                                ALU.subtract).then_inc(shifted, 1)

            def softmax_scale(i):
                dve.wait_ge(exp_done, i + 1)
                steps = Chain(dve, sm_step, i * 4 + 2)
                steps.then_wait(V.tensor_reduce(smx[:, 1, :], exl[:], AX.X, ALU.add))
                steps.then_wait(V.reciprocal(smx[:, 2, :], smx[:, 1, :]))
                wait_pairs(dve, tr4_done, i)
                V.tensor_tensor(sc[:], exl[:], smx[:, 2, :].unsqueeze(2).to_broadcast([P, TILES, E]),
                                ALU.mult).then_inc(sc_ready, 1)

            def step(t):
                for stage, lag in ((stats1, 0), (scan, 1), (softmax_shift, 2),
                                   (lambda i: norm(i, 0, xn1, tr1_done), 0), (residual, 1), (softmax_scale, 2),
                                   (clamp, 0), (lambda i: norm(i, 1, xn2, tr3_done), 1)):
                    if not isinstance(t, int) or 0 <= t - lag < PAIRS:
                        stage(t - lag)

            for t in range(4):
                step(t)
            with dve.Fori(4, PAIRS) as t:
                step(t)
            for t in range(PAIRS, PAIRS + 2):
                step(t)

            dve.wait_ge(s_ready, PAIRS)
            dve.wait_ge(wsplit_done, N_WEIGHTS)
            src, n = scores, 0

            def exchange(pair_of, k, src, dst):
                a, b = pair_of(src, k)
                oa, ob = pair_of(dst, k)
                V.tensor_tensor(oa, a, b, ALU.max).then_inc(sort_step, 1)
                V.tensor_tensor(ob, a, b, ALU.min).then_inc(sort_step, 1)

            for m, (pair_of, k) in enumerate(plan):
                exchange(pair_of, k, src, bufs[m % 2])
                n += 2
                dve.wait_ge(sort_step, n)
                src = bufs[m % 2]
            dve.wait_ge(swap_in, 64)
            V.tensor_tensor(merged_in[0:E, :], src[0:E, :], sort_c[0:E, HALF - 1::-1], ALU.max).then_inc(sort_step, 1)
            V.tensor_tensor(merged_in[E:P, :], src[E:P, :], sort_c[E:P, HALF - 1::-1], ALU.min).then_inc(sort_step, 1)
            n += 2
            dve.wait_ge(sort_step, n)
            src, dst = merged_in, src
            for pair_of, k in MERGE:
                exchange(pair_of, k, src, dst)
                n += 2
                dve.wait_ge(sort_step, n)
                src, dst = dst, src
            blocks = src[:].rearrange("p (q g) -> p q g", g=G)
            work = dst
            route = Chain(dve, route_step)
            route.add(V.tensor_reduce(gsum[:], blocks, AX.X, ALU.add))
            route.then_wait(V.tensor_reduce(gmin[:], blocks, AX.X, ALU.min))

            cur, bit, trial, hit, inc = (bits[:, k:k + 1] for k in range(5))
            cnt = rc[:, 0:1]
            route.then_wait(V.memset(cur, 0))
            route.then_wait(V.tensor_copy(bit, topbit_c.bitcast(I32)))
            base = route.n
            PER = 6
            with dve.Fori(0, 31) as i:
                route.n = base + i * PER
                route.then_wait(V.tensor_tensor(trial, cur, bit, ALU.bitwise_or))
                route.add(V.tensor_scalar(gw[:, 0, :], gsum[:], trial.bitcast(F32), None, ALU.is_ge, ALU.add,
                                          accum_out=cnt))
                dve.wait_ge(route_step, route.n)
                V.tensor_copy(rc[:, 1:2], cnt).then_inc(cnt_ready, 1)
                dve.wait_ge(cnt_summed, i + 1)
                route.then_wait(V.tensor_scalar(hit, bank[0][:, 0:1], float(BUDGET) - 0.5, None, ALU.is_ge))
                route.then_wait(V.tensor_tensor(inc, hit, bit, ALU.mult))
                route.then_wait(V.tensor_tensor(cur, cur, inc, ALU.bitwise_or))
                route.then_wait(V.tensor_scalar(bit, bit, 1, None, ALU.logical_shift_right))
            route.n = base + 31 * PER
            theta = cur.bitcast(F32)

            above, equal = gw[:, 1, :], gw[:, 2, :]
            route.then_wait(V.tensor_scalar(above, gsum[:], theta, None, ALU.is_gt, ALU.add, accum_out=rc[:, 2:3]))
            route.then_wait(V.tensor_scalar(equal, gsum[:], theta, None, ALU.is_equal, ALU.add, accum_out=rc[:, 3:4]))
            V.tensor_copy(rc[:, 4:6], rc[:, 2:4]).then_inc(tie_ready, 1)
            dve.wait_ge(tie_done, 1)
            route.then_wait(V.tensor_copy(gw[:, 3, :], bank[1][:, 0:NG]))
            route.then_wait(V.tensor_tensor_scan(gw[:, 4, :], gw[:, 3, :], gw[:, 3, :], 0.0, ALU.bypass, ALU.add)
                            if False else
                            V.tensor_tensor_scan(gw[:, 4, :], const("ones")[:, 0:NG], gw[:, 3, :], 0.0, ALU.mult, ALU.add))
            route.then_wait(V.tensor_tensor(gw[:, 4, :], gw[:, 4, :], gw[:, 3, :], ALU.subtract))
            route.then_wait(V.tensor_tensor(gw[:, 4, :], gw[:, 4, :], bank[2][:, 0:NG], ALU.add))
            route.then_wait(V.tensor_copy(rc[:, 6:8], bank[3][:, 0:2]))
            route.then_wait(V.tensor_tensor(rc[:, 12:13], rc[:, 6:7], rc[:, 7:8], ALU.add))
            route.then_wait(V.tensor_scalar(rc[:, 12:13], rc[:, 12:13], -1.0, float(BUDGET), ALU.mult, ALU.add))
            route.then_wait(V.scalar_tensor_tensor(gw[:, 5, :], gw[:, 4, :], rc[:, 12:13], equal, ALU.is_lt, ALU.mult))
            route.then_wait(V.tensor_tensor(gw[:, 5, :], gw[:, 5, :], above, ALU.add))
            V.tensor_reduce(rc[:, 13:14], gw[:, 5, :], AX.X, ALU.add).then_inc(rsum_ready, 1)
            dve.wait_ge(rsum_done, 1)
            route.then_wait(V.tensor_copy(rc[:, 14:15], bank[4][:, 0:1]))
            route.then_wait(V.tensor_scalar(gw[:, 0, :], const("rank"), rc[:, 14:15], 2.0, ALU.is_ge, ALU.mult))
            route.then_wait(V.tensor_tensor(gw[:, 0, :], gw[:, 0, :], gmin[:], ALU.max))
            V.tensor_reduce(rc[:, 8:9], gw[:, 0, :], AX.X, ALU.min).then_inc(vswap_ready, 1)
            dve.wait_ge(vswap_in, 32)
            route.then_wait(V.tensor_tensor(rc[:, 10:11], rc[:, 8:9], rc[:, 9:10], ALU.min))
            thr = rc[:, 10:11]
            eq, cum, kept = sort_a if work is sort_b else sort_b, work, sort_c
            route.add(V.tensor_scalar(kept[:], scores[:], thr, None, ALU.is_gt, ALU.add, accum_out=rc[:, 16:17]))
            route.add(V.tensor_scalar(eq[:], scores[:], thr, None, ALU.is_equal, ALU.add, accum_out=rc[:, 17:18]))
            dve.wait_ge(route_step, route.n)
            V.tensor_copy(rc[:, 18:20], rc[:, 16:18]).then_inc(rsum_ready, 1)
            dve.wait_ge(rsum_done, 2)
            route.then_wait(V.tensor_copy(rc[:, 20:22], bank[4][:, 2:4]))
            route.then_wait(V.tensor_scalar(rc[:, 22:23], rc[:, 14:15], float(G), rc[:, 20:21], ALU.mult, ALU.subtract))
            ones_row = const("ones")[:, 0:1].to_broadcast([P, HALF])
            route.then_wait(V.tensor_tensor_scan(cum[:], ones_row, eq[:], rc[:, 21:22], ALU.mult, ALU.add))
            route.then_wait(V.scalar_tensor_tensor(cum[:], cum[:], rc[:, 22:23], eq[:], ALU.is_le, ALU.mult))
            route.then_wait(V.tensor_tensor(cum[:], cum[:], kept[:], ALU.add))
            V.tensor_tensor(scores[:], cum[:], scores[:], ALU.mult).then_inc(fs_ready, 1)
            dve.wait_ge(fs_ready, 1)

            def normalise(i):
                dve.wait_ge(den_done, i + 1)
                steps = Chain(dve, den_step, i * 2)
                steps.then_wait(V.tensor_scalar(den[:, 0, :], bank[7][:, 0:L], 1e-6, None, ALU.add))
                steps.then_wait(V.reciprocal(den[:, 1, :], den[:, 0, :]))
                V.tensor_tensor(fsn[:], pair_cols(scores, i, L), den[:, 1, :], ALU.mult).then_inc(fsn_ready, 1)

            def fs_low(i):
                dve.wait_ge(fs_hi_ready, i + 1)
                dve.wait_ge(fsn_ready, i + 1)
                dst = fs2[:, bass.ds((i % 2) * PT, PT)]
                V.scalar_tensor_tensor(dst[E:P, 0:L], fsn[0:E, :], FS_SCALE, dst[0:E, 0:L], ALU.mult, ALU.subtract)
                V.scalar_tensor_tensor(dst[E:P, L:PT], fsn[E:P, :], FS_SCALE, fs_h1[E:P, :], ALU.mult,
                                       ALU.subtract).then_inc(fs2_ready, 1)

            def low_part(g, k):
                dve.wait_ge(hi_ready, g + 1)
                wait_pairs(dve, down_done, g - 3)
                V.tensor_tensor(act_lo[:, k % 4, :], act[:, k % 2, :], act_hi[:, k % 4, :],
                                ALU.subtract).then_inc(lo_ready, 1)

            def finish(i):
                dve.wait_ge(tr5_done, i + 1)
                V.tensor_tensor(pair_cols(xres, i), bank[7][:], pair_cols(xres, i), ALU.add).then_inc(fin_ready, 1)

            def experts(i, first=False, last=False):
                for k in range(CH):
                    g = i * CH + k
                    dve.wait_ge(gate_done, g + 1)
                    dve.wait_ge(silu_done, g + 1)
                    V.scalar_tensor_tensor(g1[:, k % 2, :], bank[2 + k % 2][:], bgate_c[:, k:k + 1], sl[:, k % 2, :],
                                           ALU.add, ALU.mult).then_inc(gated, 1)
                    if not (first and k == 0):
                        low_part(g - 1, (k - 1) % CH)
                    dve.wait_ge(gated, g + 1)
                    dve.wait_ge(fsb_done, g + 1)
                    V.scalar_tensor_tensor(act[:, k % 2, :], bank[4 + k % 2][:], 1.0 / (W_SCALE * FS_SCALE),
                                           g1[:, k % 2, :], ALU.mult, ALU.mult).then_inc(weighted, 1)
                    if k == 4 and not first:
                        finish(i - 1)
                    if k == 7 and not last:
                        normalise(i + 1)
                    if k == 9 and not last:
                        fs_low(i + 1)

            normalise(0)
            fs_low(0)
            experts(0, first=True)
            with dve.Fori(1, PAIRS - 1) as i:
                experts(i)
            experts(PAIRS - 1, last=True)
            low_part(PAIRS * CH - 1, CH - 1)
            finish(PAIRS - 1)

        @block.scalar
        def _(s):
            A = nc.scalar.activation
            s.dma_start(sort_a[:, 0:2048], Wup).then_inc(w_in, 16)
            s.dma_start(sort_a[:, 2048:4096], Wgate).then_inc(w_in, 16)
            s.dma_start(sort_b[:, 0:2048], Wdown).then_inc(w_in, 16)
            s.wait_ge(params_in, N_PARAMS)
            A(cs_sb[:], c_sb[:], ACT.Silu).then_inc(c_silu, 1)
            s.wait_ge(ssm_step, 1)
            A(ssm[:, 8:10], ssm[:, 4:6], ACT.Exp).then_inc(ssm_done, 1)
            s.wait_ge(ssm_done, 1)
            A(ssm[:, 10:12], ssm[:, 8:10], ACT.Ln, bias=one_c).then_inc(ssm_done, 1)
            s.wait_ge(prep_done, 1)

            def rstd_guess(i, which):
                s.wait_ge(mv_ready[which], i + 1)
                A(rstd[:, which, 0, :], mv[:, which, :, 1], ACT.Ln, bias=eps_c).then_inc(rs_step[which], 1)
                s.wait_ge(rs_step[which], i + 1)
                A(rstd[:, which, 1, :], rstd[:, which, 0, :], ACT.Exp, scale=-0.5).then_inc(rs_ready[which], 1)

            def modulate(dst, src, i, m_scale, m_shift):
                for h in range(2):
                    b = bass.ds(i + h * PAIRS, 1)
                    last = A(dst[h], src[:, h * L:(h + 1) * L], ACT.Identity, bias=m_shift[:, b], scale=m_scale[:, b])
                return last

            def affine1(i):
                s.wait_ge(tr1_done, i + 1)
                wait_pairs(s, proj_done, i)
                modulate([hT[:, h, PAD:ROW] for h in range(2)], t1_ps, i, mod[:, 1, :], mod[:, 0, :]).then_inc(h_ready, 1)

            def gates(i):
                s.wait_ge(clamped, i + 1)
                wait_pairs(s, y_ready, i)
                A(ex1[:], tcl[:], ACT.Exp, scale=expscale_c).then_inc(gate_step, 1)
                for h in range(2):
                    cut, rows = slice(h * L, (h + 1) * L), slice(h * N, (h + 1) * N)
                    A(over[rows, :], proj_ps[0:N, cut], ACT.Relu, bias=bias_p[0:N, 1:2])
                    A(ub[rows, :], u_ps[0:N, cut], ACT.Identity, bias=ssm[0:N, 16:17], scale=ssm[0:N, 13:14])
                s.wait_ge(gate_step, 2 * i + 1)
                A(ln_c[N:P, :], ex1[N:P, :], ACT.Ln, bias=one_c[N:P, :]).then_inc(gate_step, 1)
                for h in range(2):
                    cut, rows = slice(h * L, (h + 1) * L), slice(h * N, (h + 1) * N)
                    A(sp[rows, :], ex1[0:N, cut], ACT.Ln, bias=one_c[0:N, :])
                s.wait_ge(gate_step, 2 * i + 2)
                for h in range(2):
                    cut, rows = slice(h * L, (h + 1) * L), slice(h * N, (h + 1) * N)
                    last = A(qd[rows, :], ln_c[N:P, cut], ACT.Exp, scale=-1.0)
                last.then_inc(gates_ready, 1)

            def gate_attention(i):
                s.wait_ge(wo_done, i + 1)
                wait_pairs(s, tr2_done, i)
                modulate([att[:, h * L:(h + 1) * L] for h in range(2)], o_ps, i, mod[:, 2, :], ga_bo[:]).then_inc(att_ready, 1)

            def affine2(i):
                s.wait_ge(tr3_done, i + 1)
                wait_pairs(s, router_done, i)
                wait_pairs(s, split_done, i)
                modulate([h2[:, h * L:(h + 1) * L] for h in range(2)], t3_ps, i, mod[:, 4, :], mod[:, 3, :]).then_inc(h2_ready, 1)

            def softmax_exp(i):
                s.wait_ge(shifted, i + 1)
                A(exl[:], lgm[:], ACT.Exp).then_inc(exp_done, 1)

            def keep_scores(i):
                s.wait_ge(tr4_done, i + 1)
                A(pair_cols(scores, i, L), t4_ps[:, 0:L], ACT.Copy).then_inc(s_ready, 1)

            def step(t):
                for stage, lag in ((lambda i: rstd_guess(i, 0), 0), (gate_attention, 1), (softmax_exp, 2),
                                   (affine1, 0), (lambda i: rstd_guess(i, 1), 1), (keep_scores, 2),
                                   (gates, 0), (affine2, 1)):
                    if not isinstance(t, int) or 0 <= t - lag < PAIRS:
                        stage(t - lag)

            for t in range(4):
                step(t)
            with s.Fori(4, PAIRS) as t:
                step(t)
            for t in range(PAIRS, PAIRS + 2):
                step(t)

            def fs_high(i):
                s.wait_ge(fsn_ready, i + 1)
                dst = fs2[:, bass.ds((i % 2) * PT, PT)]
                A(dst[0:E, 0:L], fsn[0:E, :], ACT.Copy, scale=FS_SCALE)
                A(dst[0:E, L:PT], fsn[E:P, :], ACT.Copy, scale=FS_SCALE)
                A(fs_h1[E:P, :], fsn[E:P, :], ACT.Copy, scale=FS_SCALE).then_inc(fs_hi_ready, 1)

            def high_part(g, k):
                s.wait_ge(weighted, g + 1)
                wait_pairs(s, down_done, g - 3)
                A(act_hi[:, k % 4, :], act[:, k % 2, :], ACT.Copy).then_inc(hi_ready, 1)

            def gate_experts(i):
                s.wait_ge(out_done, i + 1)
                wait_pairs(s, tr5_done, i)
                for h in range(2):
                    last = A(oT[:, h * L:(h + 1) * L], bank[6][:, h * L:(h + 1) * L], ACT.Copy,
                             scale=mod[:, 5, bass.ds(i + h * PAIRS, 1)])
                last.then_inc(o_ready, 1)

            def experts(i, first=False, last=False):
                for k in range(CH):
                    g = i * CH + k
                    s.wait_ge(up_done, g + 1)
                    wait_pairs(s, gated, g - 1)
                    A(sl[:, k % 2, :], bank[k % 2][:], ACT.Silu, bias=bup_c[:, k:k + 1],
                      scale=1.0 / W_SCALE).then_inc(silu_done, 1)
                    if not (first and k == 0):
                        high_part(g - 1, (k - 1) % CH)
                    if k == 2 and not first:
                        gate_experts(i - 1)
                    if k == 8 and not last:
                        fs_high(i + 1)

            fs_high(0)
            experts(0, first=True)
            with s.Fori(1, PAIRS - 1) as i:
                experts(i)
            experts(PAIRS - 1, last=True)
            high_part(PAIRS * CH - 1, CH - 1)
            gate_experts(PAIRS - 1)

        @block.tensor
        def _(pe):
            M = nc.tensor.matmul
            T = nc.tensor.transpose
            pe.wait_ge(params_in, N_PARAMS)
            pe.wait_ge(c_silu, 1)
            T(bank[0][:, 0:B], cs_sb[:], ident[0:B, 0:B]).then_inc(cT_done, 1)
            M(bank[2][:, 0:1], wp_sb[:], cols[:, 0:1], start=True, stop=True).then_inc(biasp_done, 1)
            pe.wait_ge(cT_copied, 1)
            for m in range(6):
                last = M(bank[1][:, m * B:(m + 1) * B], sort_c[:, m * D:(m + 1) * D], cT[:], start=True, stop=True)
            last.then_inc(mod_done, 1)
            pe.wait_ge(prep_done, 1)
            pe.wait_ge(zeroed, 5)

            def turn1(i):
                pe.wait_ge(xn_ready[0], i + 1)
                wait_pairs(pe, h_ready, i)
                for t in range(TILES):
                    last = T(t1_ps[:, t * P:(t + 1) * P], xn1[:, t, :], ident)
                last.then_inc(tr1_done, 1)

            def project(i):
                pe.wait_ge(h_ready, i + 1)
                wait_pairs(pe, gates_ready, i)
                M(u_ps[0:N, :].rearrange("p (h t) -> p h t", h=2), ws_sb[:], hT[:, :, PAD:ROW], start=True, stop=True)
                for k in range(TAPS):
                    last = M(proj_ps[:].rearrange("p (h t) -> p h t", h=2), wtap[:, k, :], hT[:, :, k:k + L],
                             start=(k == 0), stop=(k == TAPS - 1))
                last.then_inc(proj_done, 1)

            def attention_out(i):
                pe.wait_ge(y_ready, i + 1)
                wait_pairs(pe, att_ready, i)
                M(o_ps[:, 0:L], wo_a[:], y[:], start=True, stop=True)
                M(o_ps[:, L:PT], wo_b[:], y[:], start=True, stop=True).then_inc(wo_done, 1)

            def turn2(i):
                pe.wait_ge(att_ready, i + 1)
                wait_pairs(pe, resid_done, i)
                for t in range(TILES):
                    last = T(t2_ps[:, t * P:(t + 1) * P], att[:, t * P:(t + 1) * P], ident)
                last.then_inc(tr2_done, 1)

            def turn3(i):
                pe.wait_ge(xn_ready[1], i + 1)
                wait_pairs(pe, h2_ready, i)
                for t in range(TILES):
                    last = T(t3_ps[:, t * P:(t + 1) * P], xn2[:, t, :], ident)
                last.then_inc(tr3_done, 1)

            def router(i):
                pe.wait_ge(h2_ready, i + 1)
                wait_pairs(pe, shifted, i)
                for h in range(2):
                    for p in range(TILES // 2):
                        t, k = h * (TILES // 2) + p, p * 2 + h
                        last = M(lg_ps[:, k * E:(k + 1) * E], h2[:, t * P:(t + 1) * P], wr_sb[:], start=True, stop=True)
                last.then_inc(router_done, 1)

            def turn4(i):
                pe.wait_ge(sc_ready, i + 1)
                wait_pairs(pe, s_ready, i)
                for p in range(TILES // 2):
                    last = T(t4_ps[:, p * P:(p + 1) * P], sc[:, 2 * p:2 * p + 2, :].rearrange("p t e -> p (t e)"), ident)
                last.then_inc(tr4_done, 1)

            def step(t):
                for stage, lag in ((attention_out, 1), (turn1, 0), (turn2, 1), (turn4, 2), (project, 0), (turn3, 1),
                                   (router, 1)):
                    if not isinstance(t, int) or 0 <= t - lag < PAIRS:
                        stage(t - lag)

            for t in range(4):
                step(t)
            with pe.Fori(4, PAIRS) as t:
                step(t)
            for t in range(PAIRS, PAIRS + 2):
                step(t)

            ones = const("ones")
            with pe.Fori(0, 31) as i:
                pe.wait_ge(cnt_ready, i + 1)
                M(bank[0][:, 0:1], ones, rc[:, 1:2], start=True, stop=True).then_inc(cnt_summed, 1)
            pe.wait_ge(tie_ready, 1)
            M(bank[1][:, 0:NG], const("same_half"), gw[:, 2, :], start=True, stop=True)
            M(bank[2][:, 0:NG], const("before"), gw[:, 2, :], start=True, stop=True)
            M(bank[3][:, 0:1], ones, rc[:, 4:5], start=True, stop=True)
            M(bank[3][:, 1:2], const("from_half0"), rc[:, 5:6], start=True, stop=True).then_inc(tie_done, 1)
            pe.wait_ge(rsum_ready, 1)
            M(bank[4][:, 0:1], const("pair_sum"), rc[:, 13:14], start=True, stop=True).then_inc(rsum_done, 1)
            pe.wait_ge(rsum_ready, 2)
            M(bank[4][:, 2:3], const("pair_sum"), rc[:, 18:19], start=True, stop=True)
            M(bank[4][:, 3:4], const("shift_up"), rc[:, 19:20], start=True, stop=True).then_inc(rsum_done, 1)

            pe.wait_ge(split_done, PAIRS)
            pe.wait_ge(wsplit_done, N_WEIGHTS)

            def chunk_w(t, k):
                return t[:, k * P:(k + 1) * P]

            def denominators(i):
                if not isinstance(i, int) or i > 0:
                    pe.wait_ge(fsn_ready, i)
                M(bank[7][:, 0:L], const("same_half"), pair_cols(scores, i, L), start=True, stop=True).then_inc(den_done, 1)

            def down(i, k):
                g = i * CH + k
                if k == 0:
                    wait_pairs(pe, o_ready, i)
                    M(bank[6][:, 0:L], bd_a[:], fsn[:], start=True, stop=False, skip_group_check=True)
                    M(bank[6][:, L:PT], bd_b[:], fsn[:], start=False, stop=False, skip_group_check=True)
                pe.wait_ge(lo_ready, g + 1)
                M(bank[6][:], chunk_w(down_hi, k), act_hi[:, k % 4, :], start=False, stop=False, skip_group_check=True)
                M(bank[6][:], chunk_w(down_lo, k), act_hi[:, k % 4, :], start=False, stop=False, skip_group_check=True)
                last = M(bank[6][:], chunk_w(down_hi, k), act_lo[:, k % 4, :], start=False, stop=(k == CH - 1),
                         skip_group_check=True)
                last.then_inc(down_done, 1)
                if k == CH - 1:
                    pe.wait_ge(down_done, g + 1)
                    pe.sem_inc(out_done, 1)

            def turn5(i):
                pe.wait_ge(o_ready, i + 1)
                if not isinstance(i, int) or i + 1 < PAIRS:
                    pe.wait_ge(fsn_ready, i + 2)
                for t in range(TILES):
                    last = T(bank[7][:, t * P:(t + 1) * P], oT[:, t * P:(t + 1) * P], ident)
                last.then_inc(tr5_done, 1)

            def experts(i, first=False, last=False):
                hi, lo = pair_cols(h2_hi, i), pair_cols(h2_lo, i)
                fs = fs2[:, bass.ds((i % 2) * PT, PT)]
                for k in range(CH):
                    g = i * CH + k
                    wait_pairs(pe, silu_done, g - 1)
                    M(bank[k % 2][:], chunk_w(up_hi, k), hi, start=True, stop=False)
                    M(bank[k % 2][:], chunk_w(up_hi, k), lo, start=False, stop=False)
                    M(bank[k % 2][:], chunk_w(up_lo, k), hi, start=False, stop=True).then_inc(up_done, 1)
                    wait_pairs(pe, gated, g - 1)
                    M(bank[2 + k % 2][:], chunk_w(gate_hi, k), hi, start=True, stop=False)
                    M(bank[2 + k % 2][:], chunk_w(gate_hi, k), lo, start=False, stop=False)
                    M(bank[2 + k % 2][:], chunk_w(gate_lo, k), hi, start=False, stop=True).then_inc(gate_done, 1)
                    if k == 0:
                        pe.wait_ge(fs2_ready, i + 1)
                    wait_pairs(pe, weighted, g - 1)
                    M(bank[4 + k % 2][:], chunk_w(sel, k), fs, start=True, stop=True).then_inc(fsb_done, 1)
                    if k >= 2:
                        down(i, k - 2)
                    elif not first:
                        down(i - 1, CH - 2 + k)
                    if k == 3 and not first:
                        turn5(i - 1)
                    if k == 6 and not last:
                        if not first:
                            pe.wait_ge(fin_ready, i)
                        denominators(i + 1)

            pe.wait_ge(fs_ready, 1)
            denominators(0)
            experts(0, first=True)
            with pe.Fori(1, PAIRS - 1) as i:
                experts(i)
            experts(PAIRS - 1, last=True)
            down(PAIRS - 1, CH - 2)
            down(PAIRS - 1, CH - 1)
            turn5(PAIRS - 1)


def shape_constants(np):
    p = np.arange(128)
    half, e = p // 64, p % 64
    src, dst = p[:, None], p[None, :]
    same = half[:, None] == half[None, :]
    blocks = [
        src == dst,
        np.ones((128, 128), bool),
        same,
        same & (src < dst),
        (half[:, None] == 0) & (half[None, :] == 1),
        dst == src + 64,
        e[:, None] == e[None, :],
        64 * half[:, None] + np.arange(64)[None, :],
    ]
    tail = np.zeros((128, 4))
    tail[:, 0], tail[:, 1], tail[:, 2] = 1e-5, 1.0, 2.0
    tail[:, 3] = 1.0 + half
    cst = np.concatenate([np.asarray(b, np.float32) for b in blocks] + [tail.astype(np.float32)], axis=1)
    chunk, a = np.arange(16), np.arange(128) // 32
    sel = e[:, None, None] == (4 * chunk[:, None] + a[None, :])[None]
    return cst.astype(np.float32), sel.reshape(128, 16 * 128).astype(np.float16)


def kernel(**inputs):
    import numpy as _np
    import concourse.bacc as _bacc
    from concourse import mybir as _mybir
    from concourse.bass_utils import run_bass_kernel_spmd as _run

    nc = _bacc.Bacc("TRN2", target_bir_lowering=False, num_devices=1)
    arrays, args = {}, []
    attn = {k[len("L0_attn_"):]: _np.asarray(v) for k, v in inputs.items() if k.startswith("L0_attn_")}
    ffn = {k[len("L0_ffn_"):]: _np.asarray(v) for k, v in inputs.items() if k.startswith("L0_ffn_")}
    E, D, H = ffn["Wup"].shape
    A = 128 // H

    def by_chunk(v):
        return v.reshape(E // A, A * H).T

    twice = [_np.concatenate([attn[n], attn[n]])[:, None] for n in ("bs", "A_log", "dt_log")]
    params = _np.concatenate([attn["conv_w"][:, 0].T] + [attn[n][:, None] for n in ("conv_b", "bp", "bo")] + twice
                             + [by_chunk(ffn["bup"]), by_chunk(ffn["bgate"])], axis=1)
    given = [("x", attn["x"]), ("Wp", attn["Wp"]), ("Ws", attn["Ws"]), ("Wo", attn["Wo"]), ("Wr", ffn["Wr"]),
             ("br", ffn["br"]),
             ("Wup", ffn["Wup"].transpose(1, 0, 2).reshape(D, E * H)),
             ("Wgate", ffn["Wgate"].transpose(1, 0, 2).reshape(D, E * H)),
             ("Wdown", ffn["Wdown"].reshape(E // A, A * H, D).transpose(1, 0, 2).reshape(A * H, E // A * D)),
             ("bdown", ffn["bdown"]), ("c", _np.asarray(inputs["L0_c"])), ("wmod", _np.asarray(inputs["L0_wmod"])),
             ("params", params)]
    cst, sel = shape_constants(_np)
    for name, a in given + [("consts", cst), ("selectors", sel)]:
        a = _np.ascontiguousarray(a)
        arrays[f"in_{name}"] = a
        args.append(nc.dram_tensor(f"in_{name}", a.shape, _mybir.dt.from_np(a.dtype), kind="ExternalInput").ap())
    args.append(nc.dram_tensor("out_x", (32, 256, 128), F32, kind="ExternalOutput").ap())
    adaln_kernel(nc, *args)
    r = _run(nc, [arrays], core_ids=[0])
    return r.results[0]["out_x"]
```

```python
from contextlib import ExitStack

import concourse.bass as bass
from concourse import mybir

F32 = mybir.dt.float32
F16 = mybir.dt.float16
I32 = mybir.dt.int32
ALU = mybir.AluOpType
ACT = mybir.ActivationFunctionType
AX = mybir.AxisListType

P = 128
CONSTS = ["ident", "ones", "same_half", "before", "from_half0", "shift_up", "pair_sum", "rank"]
CLAMP = 30.0
W_SCALE = 32.0
FS_SCALE = 4096.0


class Chain:

    def __init__(self, eng, sem, start=0):
        self.eng, self.sem, self.n = eng, sem, start

    def add(self, ins):
        ins.then_inc(self.sem, 1)
        self.n = self.n + 1

    def then_wait(self, ins):
        self.add(ins)
        self.eng.wait_ge(self.sem, self.n)


def wait_pairs(eng, sem, n):
    if not isinstance(n, int) or n > 0:
        eng.wait_ge(sem, n)


def adaln_kernel(nc, x, Wp, Ws, Wo, Wr, br, Wup, Wgate, Wdown, bdown, c, wmod, params, consts, sel_const, out):
    B, L, D = x.shape
    N = Ws.shape[1]
    E = Wr.shape[1]
    H = Wup.shape[1] // E
    TAPS = params.shape[1] - 6 - 2 * (E * H // P)
    PAIRS = B // 2
    PT = 2 * L
    TILES = PT // P
    HALF = PAIRS * L
    CH = E * H // P
    SLOTS, GROUP, RING = 4, 2, 8
    DIGIT, DIGITS = 7, 10
    EC = P // H
    G = 64
    BUDGET = (B * L // G) * 16
    NG = HALF // G
    EPS = 1e-5
    PAD = TAPS - 1
    ROW = L + PAD

    with ExitStack() as ctx:
        def sb(name, shape, dt=F32):
            return ctx.enter_context(nc.sbuf_tensor(name, shape, dt))

        def sem(name):
            return ctx.enter_context(nc.semaphore(name))

        bank = [ctx.enter_context(nc.psum_tensor(f"bank{k}", [P, 512], F32)) for k in range(8)]

        xres = sb("xres", [P, PAIRS * PT])
        scores = sb("scores", [P, HALF])
        h2_hi = sb("h2_hi", [P, PAIRS * PT], F16)
        h2_lo = sb("h2_lo", [P, PAIRS * PT], F16)
        cst = sb("cst", [P, 7 * P + NG + 10])
        sel = sb("sel", [P, CH * P], F16)
        up_hi, up_lo = sb("up_hi", [P, CH * P], F16), sb("up_lo", [P, CH * P], F16)
        gate_hi, gate_lo = sb("gate_hi", [P, CH * P], F16), sb("gate_lo", [P, CH * P], F16)
        down_hi, down_lo = sb("down_hi", [P, CH * P], F16), sb("down_lo", [P, CH * P], F16)
        mod = sb("mod", [P, 6, B])
        ga_bo = sb("ga_bo", [P, B])
        sort_a, sort_b, sort_c = sb("sort_a", [P, HALF]), sb("sort_b", [P, HALF]), sb("sort_c", [P, HALF])
        wtap = sb("wtap", [P, TAPS, 2 * N])
        wp_sb, ws_sb = sb("wp_sb", [P, 2 * N]), sb("ws_sb", [P, N])
        wo_a, wo_b = sb("wo_a", [P, D]), sb("wo_b", [P, D])
        wr_sb = sb("wr_sb", [P, E])
        bd_a, bd_b = sb("bd_a", [P, D]), sb("bd_b", [P, D])
        br_row = sb("br_row", [P, E])
        par = sb("par", [P, TAPS + 6 + 2 * CH])
        conv_sb, cols = par[:, 0:TAPS], par[:, TAPS:TAPS + 3]
        ssm_in = par[:, TAPS + 3:TAPS + 6]
        bup_c, bgate_c = par[:, TAPS + 6:TAPS + 6 + CH], par[:, TAPS + 6 + CH:TAPS + 6 + 2 * CH]
        ssm = sb("ssm", [P, 24])
        c_sb, cs_sb, cT = sb("c_sb", [B, D]), sb("cs_sb", [B, D]), sb("cT", [P, B])
        tmp6 = sb("tmp6", [P, 3, 2 * B])
        bias_p = sb("bias_p", [P, 2])
        decay_row = sb("decay_row", [P, L])
        tick = sb("tick", [P, 2])
        stat, mv = sb("stat", [P, 2, TILES, 6]), sb("mv", [P, 2, TILES, 2])
        rstd = sb("rstd", [P, 2, 5, TILES])
        s1_buf = [sort_c[:, 6 * D + k * PT:6 * D + (k + 1) * PT] for k in range(6)]
        xn1, xn2 = (v.rearrange("p (t d) -> p t d", d=D) for v in s1_buf[0:2])
        hT = sb("hT", [P, 2, ROW])
        tcl, ex1, ln_c = s1_buf[2:5]
        sp, over, ub, qd = sb("sp", [P, L]), sb("over", [P, 2 * L]), sb("ub", [P, 2 * L]), sb("qd", [P, L])
        cd, spo, bu, state, y = sb("cd", [P, L]), sb("spo", [P, L]), sb("bu", [P, L]), sb("state", [P, L]), sb("y", [P, L])
        att, h2 = s1_buf[5], sb("h2", [P, PT])
        lg, lgm, exl, sc = (sb(n, [P, TILES, E]) for n in ("lg", "lgm", "exl", "sc"))
        smx = sb("smx", [P, 3, TILES])
        gsum, gmin, gw = sb("gsum", [P, NG]), sb("gmin", [P, NG]), sb("gw", [P, 6, NG])
        bits = sb("bits", [P, 24], I32)
        ge = sort_c[:, 0:7 * NG].rearrange("p (d q) -> p d q", d=7)
        rc = sb("rc", [P, 44])
        g1 = sort_a[:, 0:2 * PT].rearrange("p (r t) -> p r t", r=2)
        act = sort_a[:, 4 * PT:8 * PT].rearrange("p (r t) -> p r t", r=4)
        act_hi, act_lo = (sort_b[:, k * 4 * PT:(k + 1) * 4 * PT].bitcast(F16).rearrange("p (r t) -> p r t", r=8)
                          for k in range(2))
        oT = sort_c[:, 0:PT]
        silu_ring = sb("silu_ring", [P, SLOTS, GROUP * PT])
        silu_dram = nc.dram_tensor("silu_up", (PAIRS, CH // GROUP, P, GROUP * PT), F32, kind="Internal").ap()
        fs2 = sort_c[:, 4 * PT:5 * PT].bitcast(F16)
        fsn, eq, cum, kept = (sort_c[:, PT + k * L:PT + (k + 1) * L] for k in range(4))
        den, rden = sb("den", [P, TILES]), sb("rden", [P, 2 * TILES])
        fs_h1 = sort_c[:, 5 * PT:5 * PT + L // 2].bitcast(F16)

        def const(name):
            k = CONSTS.index(name)
            return cst[:, k * P:(k + 1) * P] if name != "rank" else cst[:, k * P:k * P + NG]
        eps_c = cst[:, 7 * P + NG:7 * P + NG + 1]
        one_c = cst[:, 7 * P + NG + 1:7 * P + NG + 2]
        expscale_c = cst[:, 7 * P + NG + 2:7 * P + NG + 3]
        topdigit_c = cst[:, 7 * P + NG + 3:7 * P + NG + 10]
        ident = const("ident")

        params_in, w_in, br_in, x_in, x_half = (sem(n) for n in ("params_in", "w_in", "br_in", "x_in", "x_half"))
        c_silu, cT_done, cT_copied, mod_done = (sem(n) for n in ("c_silu", "cT_done", "cT_copied", "mod_done"))
        biasp_done, setup_step, prep_done, ssm_step, ssm_done = (
            sem(n) for n in ("biasp_done", "setup_step", "prep_done", "ssm_step", "ssm_done"))
        zeroed, wsplit_step, wsplit_done = sem("zeroed"), sem("wsplit_step"), sem("wsplit_done")
        mv_ready, rs_step, rs_ready = ([sem(f"{n}{k}") for k in (1, 2)] for n in ("mv_ready", "rs_step", "rs_ready"))
        stat_step, norm_step, xn_ready = ([sem(f"{n}{k}") for k in (1, 2)] for n in ("stat_step", "norm_step", "xn_ready"))
        tr1_done, h_ready, proj_done, clamped, gate_step, gates_ready, psum_taken = (
            sem(n) for n in ("tr1_done", "h_ready", "proj_done", "clamped", "gate_step", "gates_ready", "psum_taken"))
        scan_step, y_ready, wo_done, att_ready, tr2_done, resid_done = (
            sem(n) for n in ("scan_step", "y_ready", "wo_done", "att_ready", "tr2_done", "resid_done"))
        tr3_done, h2_ready, split_step, split_done, router_done = (
            sem(n) for n in ("tr3_done", "h2_ready", "split_step", "split_done", "router_done"))
        sm_step, shifted, exp_done, norm_done, sc_ready, tr4_done, s_ready = (
            sem(n) for n in ("sm_step", "shifted", "exp_done", "norm_done", "sc_ready", "tr4_done", "s_ready"))
        sort_step, swap_in, route_step, cnt_ready, cnt_summed = (
            sem(n) for n in ("sort_step", "swap_in", "route_step", "cnt_ready", "cnt_summed"))
        tie_ready, tie_done, rsum_ready, rsum_done, vswap_ready, vswap_in, fs_ready = (
            sem(n) for n in ("tie_ready", "tie_done", "rsum_ready", "rsum_done", "vswap_ready", "vswap_in", "fs_ready"))
        choose_step, rden_ready = sem("choose_step"), sem("rden_ready")
        den_done, den_step, fsn_ready, fs_hi_ready, fs2_ready = (
            sem(n) for n in ("den_done", "den_step", "fsn_ready", "fs_hi_ready", "fs2_ready"))
        spilled, loaded = ([sem(f"{n}{k}") for k in range(SLOTS)] for n in ("spilled", "loaded"))
        up_done, gate_done, fsb_done, silu_done, gated, weighted, hi_ready, lo_ready, down_done = (
            sem(n) for n in ("up_done", "gate_done", "fsb_done", "silu_done", "gated", "weighted", "hi_ready",
                             "lo_ready", "down_done"))
        out_done, o_ready, tr5_done, fin_ready, stored = (
            sem(n) for n in ("out_done", "o_ready", "tr5_done", "fin_ready", "stored"))

        x_view = x.rearrange("(h j) (s p) d -> j h p s d", h=2, p=P)
        out_view = out.rearrange("(h j) (s p) d -> j h p s d", h=2, p=P)

        def pair_cols(t, i, w=PT):
            return t[:, bass.ds(i * w, w)]

        N_PARAMS = 16 * 13
        N_WEIGHTS = 3

        bufs = [sort_a, sort_b]

        def flip(t, k):
            v = t[:].rearrange("p (n k) -> p n k", k=k)
            return v[:, :, 0:k // 2], v[:, :, k - 1:k // 2 - 1:-1] if k > 2 else v[:, :, 1:2]

        def apart(t, j):
            v = t[:].rearrange("p (n a j) -> p n a j", a=2, j=j)
            return v[:, :, 0, :], v[:, :, 1, :]

        plan = []
        k = 2
        while k <= HALF:
            plan.append((flip, k))
            j = k // 4
            while j >= 1:
                plan.append((apart, j))
                j //= 2
            k *= 2
        MERGE = []
        j = HALF // 2
        while j >= G:
            MERGE.append((apart, j))
            j //= 2
        SORTED = 2 * len(plan)
        sorted_in = bufs[(len(plan) - 1) % 2]
        merged_in = bufs[len(plan) % 2]

        DEEPEST = 7

        def run_pairs(eng, stages):
            def step(t):
                for stage, lag in stages:
                    if not isinstance(t, int) or 0 <= t - lag < PAIRS:
                        stage(t - lag)

            for t in range(DEEPEST + 1):
                step(t)
            with eng.Fori(DEEPEST + 1, PAIRS) as t:
                step(t)
            for t in range(PAIRS, PAIRS + DEEPEST):
                step(t)

        def run_experts(eng, experts):
            experts(0, 0, first=True)
            with eng.Fori(0, (PAIRS - 2) // 2) as j:
                experts(2 * j + 1, 1)
                experts(2 * j + 2, 0)
            experts(PAIRS - 1, 1, last=True)

        block = ctx.enter_context(nc.Block())

        @block.sync
        def _(sp_eng):
            def load(dst, src):
                sp_eng.dma_start(dst, src).then_inc(params_in, 16)

            load(cst[:], consts)
            load(c_sb[:], c)
            load(sort_c[:, 0:6 * D], wmod)
            load(wp_sb[:], Wp)
            load(ws_sb[:], Ws)
            load(wr_sb[:], Wr)
            load(par[:], params)
            load(br_row[:], br.partition_broadcast(P))
            load(sel[:], sel_const)
            load(wo_a[0:N, :], Wo)
            load(wo_b[N:P, :], Wo)
            load(bd_a[0:E, :], bdown)
            load(bd_b[E:P, :], bdown)
            def load_pair(i):
                for h in range(2):
                    sp_eng.dma_start(pair_cols(xres, i)[:, h * L:(h + 1) * L].rearrange("p (s d) -> p s d", d=D),
                                     x_view[bass.ds(i, 1), h].rearrange("a p s d -> (a p) s d")).then_inc(x_in, 16)

            load_pair(0)
            with sp_eng.Fori(1, PAIRS) as i:
                sp_eng.wait_ge(x_in, 32 * i)
                load_pair(i)
            with sp_eng.Fori(0, PAIRS) as i:
                for q in range(CH // GROUP):
                    sp_eng.wait_ge(silu_done, i * CH + (q + 1) * GROUP)
                    sp_eng.dma_start(silu_dram[bass.ds(i, 1), q].rearrange("a p n -> (a p) n"),
                                     silu_ring[:, q % SLOTS, :]).then_inc(spilled[q % SLOTS], 16)
            for q in range(SLOTS):
                sp_eng.wait_ge(spilled[q], 16 * PAIRS * CH // GROUP // SLOTS)

            def load_silu(i, q):
                sp_eng.dma_start(silu_ring[:, q % SLOTS, :],
                                 silu_dram[bass.ds(i, 1), q].rearrange("a p n -> (a p) n")).then_inc(loaded[q % SLOTS], 16)

            for q in range(SLOTS):
                load_silu(0, q)
            for piece in range(2):
                cut = slice(piece * HALF // 2, (piece + 1) * HALF // 2)
                if piece == 0:
                    sp_eng.wait_ge(sort_step, SORTED)
                sp_eng.dma_start(sort_c[0:E, cut], sorted_in[E:P, cut]).then_inc(swap_in, 16)
                sp_eng.dma_start(sort_c[E:P, cut], sorted_in[0:E, cut]).then_inc(swap_in, 16)
            sp_eng.wait_ge(vswap_ready, 1)
            sp_eng.dma_start(rc[0:E, 9:10], rc[E:P, 8:9]).then_inc(vswap_in, 16)
            sp_eng.dma_start(rc[E:P, 9:10], rc[0:E, 8:9]).then_inc(vswap_in, 16)
            def load_pair_silu(i, first_q):
                for q in range(first_q, CH // GROUP):
                    sp_eng.wait_ge(gated, i * CH + (q + 1 - SLOTS) * GROUP)
                    load_silu(i, q)

            load_pair_silu(0, SLOTS)
            with sp_eng.Fori(1, PAIRS) as i:
                load_pair_silu(i, 0)

        t1_ps, proj_ps, u_ps, o_ps, t2_ps, t3_ps, lg_ps, t4_ps = bank

        @block.gpsimd
        def _(pool):
            zeros = Chain(pool, zeroed)
            for t in (wo_a[N:P, :], wo_b[0:N, :], bd_a[E:P, :], bd_b[0:E, :], hT[:]):
                zeros.then_wait(nc.gpsimd.memset(t, 0.0))
            steps = Chain(pool, wsplit_step)
            pool.wait_ge(w_in, 48)
            raw = [(sort_a[:, 0:2048], up_hi, up_lo), (sort_a[:, 2048:4096], gate_hi, gate_lo),
                   (sort_b[:, 0:2048], down_hi, down_lo)]
            for raw_k, (w, hi, lo) in enumerate(raw):
                steps.then_wait(nc.gpsimd.tensor_scalar(w, w, W_SCALE, None, ALU.mult))
                steps.then_wait(nc.gpsimd.tensor_copy(hi[:], w))
                nc.gpsimd.tensor_tensor(lo[:], w, hi[:], ALU.subtract).then_inc(wsplit_done, 1)
                pool.wait_ge(wsplit_done, raw_k + 1)
            with pool.Fori(0, PAIRS) as i:
                pool.wait_ge(h2_ready, i + 1)
                nc.gpsimd.tensor_copy(pair_cols(h2_hi, i), h2[:]).then_inc(split_step, 1)
                pool.wait_ge(split_step, i + 1)
                nc.gpsimd.tensor_tensor(pair_cols(h2_lo, i), h2[:], pair_cols(h2_hi, i),
                                        ALU.subtract).then_inc(split_done, 1)
                pool.wait_ge(split_done, i + 1)

            def low_part(g, k):
                pool.wait_ge(hi_ready, g + 1)
                wait_pairs(pool, down_done, g + 1 - RING)
                nc.gpsimd.tensor_tensor(act_lo[:, k % RING, :], act[:, k % 4, :], act_hi[:, k % RING, :],
                                        ALU.subtract).then_inc(lo_ready, 1)
                pool.wait_ge(lo_ready, g + 1)

            for k in range(RING):
                low_part(k, k)
            with pool.Fori(1, PAIRS * CH // RING) as j:
                for k in range(RING):
                    low_part(j * RING + k, k)

        @block.vector
        def _(dve):
            V = nc.vector
            setup = Chain(dve, setup_step)
            dve.wait_ge(params_in, N_PARAMS)
            for k in range(TAPS):
                setup.add(V.tensor_scalar(wtap[:, k, :], wp_sb[:], conv_sb[:, k:k + 1], None, ALU.mult))
            setup.add(V.tensor_scalar(ssm[:, 4:6], ssm_in[:, 1:3], CLAMP, None, ALU.min))
            V.tensor_scalar(ssm[:, 6:8], ssm_in[:, 1:3], CLAMP, 0.0, ALU.subtract, ALU.max).then_inc(ssm_step, 1)
            dve.wait_ge(ssm_done, 2)
            dve.wait_ge(ssm_step, 1)
            setup.then_wait(V.tensor_tensor(ssm[:, 12:14], ssm[:, 6:8], ssm[:, 10:12], ALU.add))
            setup.then_wait(V.tensor_tensor(ssm[:, 14:15], ssm[:, 12:13], ssm[:, 13:14], ALU.mult))
            setup.then_wait(V.tensor_scalar(ssm[:, 15:16], ssm[:, 14:15], -1.0, 1.0, ALU.mult, ALU.add))
            setup.then_wait(V.memset(decay_row[:], 0.0))
            setup.then_wait(V.tensor_scalar(decay_row[:], decay_row[:], ssm[:, 15:16], None, ALU.add))
            setup.then_wait(V.tensor_tensor(ssm[:, 16:17], ssm_in[:, 0:1], ssm[:, 13:14], ALU.mult))
            dve.wait_ge(cT_done, 1)
            V.tensor_copy(cT[:], bank[0][:, 0:B]).then_inc(cT_copied, 1)
            dve.wait_ge(mod_done, 1)
            setup.then_wait(V.tensor_copy(mod[:], bank[1][:, 0:6 * B].rearrange("p (m b) -> p m b", b=B)))
            for m in (1, 4):
                setup.then_wait(V.tensor_scalar(mod[:, m, :], mod[:, m, :], 1.0, None, ALU.add))
            for m in (2, 5):
                setup.then_wait(V.tensor_scalar(tmp6[:, 0, 0:B], mod[:, m, :], 0.0, 2.0, ALU.is_ge, ALU.mult))
                setup.then_wait(V.tensor_scalar(tmp6[:, 1, 0:B], mod[:, m, :], -1.0, None, ALU.mult))
                setup.then_wait(V.tensor_tensor(tmp6[:, 2, 0:B], mod[:, m, :], tmp6[:, 1, 0:B], ALU.max))
                setup.then_wait(V.tensor_scalar(tmp6[:, 2, 0:B], tmp6[:, 2, 0:B], 0.25, None, ALU.max))
                setup.then_wait(V.tensor_scalar(tmp6[:, 0, 0:B], tmp6[:, 0, 0:B], 1.0, None, ALU.subtract))
                setup.then_wait(V.tensor_tensor(mod[:, m, :], tmp6[:, 2, 0:B], tmp6[:, 0, 0:B], ALU.mult))
            setup.then_wait(V.tensor_scalar(ga_bo[:], mod[:, 2, :], cols[:, 2:3], None, ALU.mult))
            setup.then_wait(V.tensor_scalar(mod[:, 5, :], mod[:, 5, :], 1.0 / W_SCALE, None, ALU.mult))
            setup.then_wait(V.tensor_scalar(bgate_c[:], bgate_c[:], W_SCALE, None, ALU.mult))
            dve.wait_ge(zeroed, 5)
            setup.then_wait(V.tensor_scalar(bd_a[:], bd_a[:], W_SCALE, None, ALU.mult))
            setup.then_wait(V.tensor_scalar(bd_b[:], bd_b[:], W_SCALE, None, ALU.mult))
            dve.wait_ge(biasp_done, 1)
            setup.then_wait(V.tensor_tensor(bias_p[:, 0:1], bank[2][:, 0:1], cols[:, 1:2], ALU.add))
            V.tensor_scalar(bias_p[:, 1:2], bias_p[:, 0:1], CLAMP, None, ALU.subtract).then_inc(prep_done, 1)

            def stats(i, which):
                v = pair_cols(xres, i).rearrange("p (t d) -> p t d", d=D)
                steps = Chain(dve, stat_step[which], i * TILES)
                V.memset(tick[:, 0:1], 0.0)
                for t in range(TILES):
                    steps.add(V.bn_stats(stat[:, which, t, :], v[:, t, :]))
                dve.wait_ge(stat_step[which], steps.n)
                V.memset(tick[:, 1:2], 0.0)
                for t in range(TILES):
                    last = V.bn_aggr(mv[:, which, t, :], stat[:, which, t, :])
                last.then_inc(mv_ready[which], 1)

            def stats1(i):
                dve.wait_ge(x_in, 32 * i + 32)
                stats(i, 0)

            def norm(i, which, xn, xn_read):
                v = pair_cols(xres, i).rearrange("p (t d) -> p t d", d=D)
                r, var = rstd[:, which], mv[:, which, :, 1]
                dve.wait_ge(rs_ready[which], i + 1)
                steps = Chain(dve, norm_step[which], i * 4)
                steps.then_wait(V.tensor_tensor(r[:, 2, :], r[:, 1, :], r[:, 1, :], ALU.mult))
                steps.then_wait(V.scalar_tensor_tensor(r[:, 3, :], var, EPS, r[:, 2, :], ALU.add, ALU.mult))
                steps.then_wait(V.tensor_scalar(r[:, 2, :], r[:, 3, :], -0.5, 1.5, ALU.mult, ALU.add))
                steps.then_wait(V.tensor_tensor(r[:, 4, :], r[:, 1, :], r[:, 2, :], ALU.mult))
                wait_pairs(dve, xn_read, i)
                for t in range(TILES):
                    last = V.tensor_scalar(xn[:, t, :], v[:, t, :], mv[:, which, t, 0:1], r[:, 4, t:t + 1],
                                           ALU.subtract, ALU.mult)
                last.then_inc(xn_ready[which], 1)

            def clamp(i):
                dve.wait_ge(proj_done, i + 1)
                wait_pairs(dve, gate_step, 2 * i - 1)
                V.tensor_scalar(tcl[:], proj_ps[:], bias_p[:, 0:1], CLAMP, ALU.add, ALU.min).then_inc(clamped, 1)

            def scan(i):
                dve.wait_ge(gates_ready, i + 1)
                steps = Chain(dve, scan_step, i * 4)
                steps.add(V.tensor_scalar(cd[:], qd[:], -2.0, 1.0, ALU.mult, ALU.add))
                steps.then_wait(V.tensor_tensor(spo[:], sp[:], pair_cols(over, i % 2, L), ALU.add))
                steps.then_wait(V.tensor_tensor(bu[:], spo[:], pair_cols(ub, i % 2, L), ALU.mult))
                steps.then_wait(V.tensor_tensor_scan(state[:], decay_row[:], bu[:], 0.0, ALU.mult, ALU.add))
                wait_pairs(dve, wo_done, i)
                V.tensor_tensor(y[:], cd[:], state[:], ALU.mult).then_inc(y_ready, 1)

            def residual(i):
                dve.wait_ge(tr2_done, i + 1)
                V.tensor_tensor(pair_cols(xres, i), t2_ps[:], pair_cols(xres, i), ALU.add).then_inc(resid_done, 1)
                dve.wait_ge(resid_done, i + 1)
                stats(i, 1)

            def softmax_shift(i):
                dve.wait_ge(router_done, i + 1)
                steps = Chain(dve, sm_step, i * 4)
                steps.then_wait(V.tensor_tensor(lg[:], lg_ps[:, 0:TILES * E].rearrange("p (t e) -> p t e", e=E),
                                                br_row[:].unsqueeze(1).to_broadcast([P, TILES, E]), ALU.add))
                steps.then_wait(V.tensor_reduce(smx[:, 0, :], lg[:], AX.X, ALU.max))
                V.tensor_tensor(lgm[:], lg[:], smx[:, 0, :].unsqueeze(2).to_broadcast([P, TILES, E]),
                                ALU.subtract).then_inc(shifted, 1)

            def softmax_scale(i):
                dve.wait_ge(exp_done, i + 1)
                steps = Chain(dve, sm_step, i * 4 + 2)
                steps.then_wait(V.tensor_reduce(smx[:, 1, :], exl[:], AX.X, ALU.add))
                steps.then_wait(V.reciprocal(smx[:, 2, :], smx[:, 1, :]))
                wait_pairs(dve, tr4_done, i)
                V.tensor_tensor(sc[:], exl[:], smx[:, 2, :].unsqueeze(2).to_broadcast([P, TILES, E]),
                                ALU.mult).then_inc(sc_ready, 1)

            run_pairs(dve, ((lambda i: norm(i, 0, xn1, tr1_done), 1), (clamp, 2), (scan, 3),
                            (lambda i: norm(i, 1, xn2, tr3_done), 5), (softmax_scale, 7), (softmax_shift, 6),
                            (residual, 4), (stats1, 0)))

            dve.wait_ge(s_ready, PAIRS)
            dve.wait_ge(wsplit_done, N_WEIGHTS)
            src, n = scores, 0

            def exchange(pair_of, k, src, dst):
                a, b = pair_of(src, k)
                oa, ob = pair_of(dst, k)
                V.tensor_tensor(oa, a, b, ALU.max).then_inc(sort_step, 1)
                V.tensor_tensor(ob, a, b, ALU.min).then_inc(sort_step, 1)

            for m, (pair_of, k) in enumerate(plan):
                exchange(pair_of, k, src, bufs[m % 2])
                n += 2
                dve.wait_ge(sort_step, n)
                src = bufs[m % 2]
            dve.wait_ge(swap_in, 64)
            V.tensor_tensor(merged_in[0:E, :], src[0:E, :], sort_c[0:E, HALF - 1::-1], ALU.max).then_inc(sort_step, 1)
            V.tensor_tensor(merged_in[E:P, :], src[E:P, :], sort_c[E:P, HALF - 1::-1], ALU.min).then_inc(sort_step, 1)
            n += 2
            dve.wait_ge(sort_step, n)
            src, dst = merged_in, src
            for pair_of, k in MERGE:
                exchange(pair_of, k, src, dst)
                n += 2
                dve.wait_ge(sort_step, n)
                src, dst = dst, src
            blocks = src[:].rearrange("p (q g) -> p q g", g=G)
            work = dst
            route = Chain(dve, route_step)
            route.add(V.tensor_reduce(gsum[:], blocks, AX.X, ALU.add))
            route.then_wait(V.tensor_reduce(gmin[:], blocks, AX.X, ALU.min))

            cur, bit, inc = (bits[:, k:k + 1] for k in range(3))
            digit_bits, trials = bits[:, 8:8 + DIGIT], bits[:, 16:16 + DIGIT]
            route.then_wait(V.memset(cur, 0))
            route.then_wait(V.tensor_copy(digit_bits, topdigit_c.bitcast(I32)))

            def search(i, n_trials, shift):
                tr, db = trials[:, 0:n_trials], digit_bits[:, 0:n_trials]
                route.then_wait(V.tensor_tensor(tr, db, cur.to_broadcast([P, n_trials]), ALU.bitwise_or))
                route.then_wait(V.tensor_tensor(ge[:, 0:n_trials, :], gsum[:].unsqueeze(1).to_broadcast([P, n_trials, NG]),
                                                tr.bitcast(F32).unsqueeze(2).to_broadcast([P, n_trials, NG]), ALU.is_ge))
                V.tensor_reduce(rc[:, 24:24 + n_trials], ge[:, 0:n_trials, :], AX.X, ALU.add).then_inc(cnt_ready, 1)
                dve.wait_ge(cnt_summed, i + 1)
                route.add(V.tensor_scalar(rc[:, 32:32 + n_trials], bank[0][:, 0:n_trials], float(BUDGET) - 0.5, None,
                                          ALU.is_ge, ALU.add, accum_out=rc[:, 40:41]))
                dve.wait_ge(route_step, route.n)
                route.then_wait(V.tensor_tensor(inc, rc[:, 40:41], digit_bits[:, 0:1], ALU.mult))
                route.then_wait(V.tensor_tensor(cur, cur, inc, ALU.bitwise_or))
                route.then_wait(V.tensor_scalar(digit_bits, digit_bits, shift, None, ALU.logical_shift_right))

            base = route.n
            PER = 6
            with dve.Fori(0, DIGITS) as i:
                route.n = base + i * PER
                search(i, DIGIT, 3)
            route.n = base + DIGITS * PER
            route.then_wait(V.memset(digit_bits, 1))
            search(DIGITS, 1, 0)
            theta = cur.bitcast(F32)

            above, equal = gw[:, 1, :], gw[:, 2, :]
            route.then_wait(V.tensor_scalar(above, gsum[:], theta, None, ALU.is_gt, ALU.add, accum_out=rc[:, 2:3]))
            route.then_wait(V.tensor_scalar(equal, gsum[:], theta, None, ALU.is_equal, ALU.add, accum_out=rc[:, 3:4]))
            V.tensor_copy(rc[:, 4:6], rc[:, 2:4]).then_inc(tie_ready, 1)
            dve.wait_ge(tie_done, 1)
            route.then_wait(V.tensor_copy(gw[:, 3, :], bank[1][:, 0:NG]))
            route.then_wait(V.tensor_tensor_scan(gw[:, 4, :], gw[:, 3, :], gw[:, 3, :], 0.0, ALU.bypass, ALU.add)
                            if False else
                            V.tensor_tensor_scan(gw[:, 4, :], const("ones")[:, 0:NG], gw[:, 3, :], 0.0, ALU.mult, ALU.add))
            route.then_wait(V.tensor_tensor(gw[:, 4, :], gw[:, 4, :], gw[:, 3, :], ALU.subtract))
            route.then_wait(V.tensor_tensor(gw[:, 4, :], gw[:, 4, :], bank[2][:, 0:NG], ALU.add))
            route.then_wait(V.tensor_copy(rc[:, 6:8], bank[3][:, 0:2]))
            route.then_wait(V.tensor_tensor(rc[:, 12:13], rc[:, 6:7], rc[:, 7:8], ALU.add))
            route.then_wait(V.tensor_scalar(rc[:, 12:13], rc[:, 12:13], -1.0, float(BUDGET), ALU.mult, ALU.add))
            route.then_wait(V.scalar_tensor_tensor(gw[:, 5, :], gw[:, 4, :], rc[:, 12:13], equal, ALU.is_lt, ALU.mult))
            route.then_wait(V.tensor_tensor(gw[:, 5, :], gw[:, 5, :], above, ALU.add))
            V.tensor_reduce(rc[:, 13:14], gw[:, 5, :], AX.X, ALU.add).then_inc(rsum_ready, 1)
            dve.wait_ge(rsum_done, 1)
            route.then_wait(V.tensor_copy(rc[:, 14:15], bank[4][:, 0:1]))
            route.then_wait(V.tensor_scalar(gw[:, 0, :], const("rank"), rc[:, 14:15], 2.0, ALU.is_ge, ALU.mult))
            route.then_wait(V.tensor_tensor(gw[:, 0, :], gw[:, 0, :], gmin[:], ALU.max))
            V.tensor_reduce(rc[:, 8:9], gw[:, 0, :], AX.X, ALU.min).then_inc(vswap_ready, 1)
            dve.wait_ge(vswap_in, 32)
            route.then_wait(V.tensor_tensor(rc[:, 10:11], rc[:, 8:9], rc[:, 9:10], ALU.min))
            thr = rc[:, 10:11]
            route.add(V.tensor_scalar(work[:], scores[:], thr, None, ALU.is_gt, ALU.add, accum_out=rc[:, 16:17]))
            route.add(V.tensor_scalar(src[:], scores[:], thr, None, ALU.is_equal, ALU.add, accum_out=rc[:, 17:18]))
            dve.wait_ge(route_step, route.n)
            V.tensor_copy(rc[:, 18:20], rc[:, 16:18]).then_inc(rsum_ready, 1)
            dve.wait_ge(rsum_done, 2)
            route.then_wait(V.tensor_copy(rc[:, 20:22], bank[4][:, 2:4]))
            V.tensor_scalar(rc[:, 22:23], rc[:, 14:15], float(G), rc[:, 20:21], ALU.mult,
                            ALU.subtract).then_inc(fs_ready, 1)
            dve.wait_ge(fs_ready, 1)
            ties_seen, ties_wanted = rc[:, 21:22], rc[:, 22:23]

            def choose(i, part):
                s_i = pair_cols(scores, i, L)
                if part > 0:
                    dve.wait_ge(choose_step, i * 5 + part)
                if part == 0:
                    V.tensor_scalar(eq[:], s_i, thr, None, ALU.is_equal).then_inc(choose_step, 1)
                elif part == 1:
                    V.tensor_tensor_scan(cum[:], const("ones")[:, 0:1].to_broadcast([P, L]), eq[:], ties_seen,
                                         ALU.mult, ALU.add).then_inc(choose_step, 1)
                elif part == 2:
                    V.tensor_copy(ties_seen, cum[:, L - 1:L]).then_inc(choose_step, 1)
                elif part == 3:
                    V.scalar_tensor_tensor(eq[:], cum[:], ties_wanted, eq[:], ALU.is_le, ALU.mult).then_inc(choose_step, 1)
                elif part == 4:
                    V.scalar_tensor_tensor(kept[:], s_i, thr, eq[:], ALU.is_gt, ALU.add).then_inc(choose_step, 1)
                else:
                    if not isinstance(i, int) or i > 0:
                        dve.wait_ge(down_done, (i - 1) * CH + 1)
                    V.tensor_tensor(fsn[:], kept[:], s_i, ALU.mult).then_inc(fsn_ready, 1)

            def denominator(i, par):
                dve.wait_ge(den_done, i + 1)
                r = rden[:, par * TILES:(par + 1) * TILES]
                V.tensor_scalar(den[:], bank[6 + par][:, 0:TILES], 1e-6, None, ALU.add).then_inc(den_step, 1)
                dve.wait_ge(den_step, i + 1)
                V.reciprocal(r, den[:]).then_inc(rden_ready, 1)

            def fs_low(i, par):
                dve.wait_ge(fs_hi_ready, i + 1)
                dve.wait_ge(fsn_ready, i + 1)
                dst = fs2[:, par * PT:(par + 1) * PT]
                V.scalar_tensor_tensor(dst[E:P, 0:L], fsn[0:E, :], FS_SCALE, dst[0:E, 0:L], ALU.mult, ALU.subtract)
                V.scalar_tensor_tensor(dst[E:P, L:PT], fsn[E:P, :], FS_SCALE, fs_h1[E:P, :], ALU.mult,
                                       ALU.subtract).then_inc(fs2_ready, 1)

            def finish(i, par, tiles):
                dve.wait_ge(tr5_done, i + 1)
                dve.wait_ge(rden_ready, i + 1)
                v, r = pair_cols(xres, i), rden[:, par * TILES:(par + 1) * TILES]
                for t in tiles:
                    h, p = t // 2, t % 2
                    cut = slice(t * P, (t + 1) * P)
                    last = V.scalar_tensor_tensor(v[:, cut], bank[6 + par][:, cut], r[:, 2 * p + h:2 * p + h + 1], v[:, cut],
                                                  ALU.mult, ALU.add)
                if TILES - 1 in tiles:
                    last.then_inc(fin_ready, 1)

            def experts(i, par, first=False, last=False):
                for k in range(CH):
                    g = i * CH + k
                    q = k // GROUP
                    dve.wait_ge(gate_done, g + 1)
                    if k % GROUP == 0:
                        dve.wait_ge(loaded[q % SLOTS], 16 * (i * (CH // GROUP // SLOTS) + q // SLOTS + 1))
                    V.scalar_tensor_tensor(g1[:, k % 2, :], bank[k % 4][:], bgate_c[:, k:k + 1],
                                           silu_ring[:, q % SLOTS, (k % GROUP) * PT:(k % GROUP + 1) * PT],
                                           ALU.add, ALU.mult).then_inc(gated, 1)
                    if 5 <= k <= 10 and not last:
                        choose(i + 1, k - 5)
                    if k in (6, 7) and not first:
                        finish(i - 1, 1 - par, range(2 * (k - 6), 2 * (k - 6) + 2))
                    if k == 13 and not last:
                        denominator(i + 1, 1 - par)
                    if k == 12 and not last:
                        fs_low(i + 1, 1 - par)
                    dve.wait_ge(gated, g + 1)
                    dve.wait_ge(fsb_done, g + 1)
                    wait_pairs(dve, lo_ready, g - 3)
                    V.scalar_tensor_tensor(act[:, k % 4, :], bank[4 + k % 2][:], 1.0 / (W_SCALE * FS_SCALE),
                                           g1[:, k % 2, :], ALU.mult, ALU.mult).then_inc(weighted, 1)

            for part in range(6):
                choose(0, part)
            fs_low(0, 0)
            denominator(0, 0)
            run_experts(dve, experts)
            finish(PAIRS - 1, 1, range(TILES))

        @block.scalar
        def _(s):
            A = nc.scalar.activation
            s.dma_start(sort_a[:, 0:2048], Wup).then_inc(w_in, 16)
            s.dma_start(sort_a[:, 2048:4096], Wgate).then_inc(w_in, 16)
            s.dma_start(sort_b[:, 0:2048], Wdown).then_inc(w_in, 16)
            s.wait_ge(params_in, N_PARAMS)
            A(cs_sb[:], c_sb[:], ACT.Silu).then_inc(c_silu, 1)
            s.preload_act_table_set("natural_log_exp_and_others")
            s.wait_ge(ssm_step, 1)
            A(ssm[:, 8:10], ssm[:, 4:6], ACT.Exp).then_inc(ssm_done, 1)
            s.wait_ge(ssm_done, 1)
            A(ssm[:, 10:12], ssm[:, 8:10], ACT.Ln, bias=one_c).then_inc(ssm_done, 1)
            s.wait_ge(prep_done, 1)

            def rstd_guess(i, which):
                s.wait_ge(mv_ready[which], i + 1)
                A(rstd[:, which, 0, :], mv[:, which, :, 1], ACT.Ln, bias=eps_c).then_inc(rs_step[which], 1)
                s.wait_ge(rs_step[which], i + 1)
                A(rstd[:, which, 1, :], rstd[:, which, 0, :], ACT.Exp, scale=-0.5).then_inc(rs_ready[which], 1)

            def modulate(dst, src, i, m_scale, m_shift):
                for h in range(2):
                    b = bass.ds(i + h * PAIRS, 1)
                    last = A(dst[h], src[:, h * L:(h + 1) * L], ACT.Identity, bias=m_shift[:, b], scale=m_scale[:, b])
                return last

            def affine1(i):
                s.wait_ge(tr1_done, i + 1)
                wait_pairs(s, proj_done, i)
                modulate([hT[:, h, PAD:ROW] for h in range(2)], t1_ps, i, mod[:, 1, :], mod[:, 0, :]).then_inc(h_ready, 1)

            def take_psum(i):
                s.wait_ge(proj_done, i + 1)
                wait_pairs(s, y_ready, i - 1)
                for h in range(2):
                    cut, rows = slice(h * L, (h + 1) * L), slice(h * N, (h + 1) * N)
                    A(pair_cols(ub, i % 2, L)[rows, :], u_ps[0:N, cut], ACT.Identity, bias=ssm[0:N, 16:17],
                      scale=ssm[0:N, 13:14])
                s.wait_ge(clamped, i + 1)
                for h in range(2):
                    cut, rows = slice(h * L, (h + 1) * L), slice(h * N, (h + 1) * N)
                    last = A(pair_cols(over, i % 2, L)[rows, :], proj_ps[0:N, cut], ACT.Relu, bias=bias_p[0:N, 1:2])
                last.then_inc(psum_taken, 1)

            def gates(i):
                A(ex1[:], tcl[:], ACT.Exp, scale=expscale_c).then_inc(gate_step, 1)
                s.wait_ge(gate_step, 2 * i + 1)
                A(ln_c[N:P, :], ex1[N:P, :], ACT.Ln, bias=one_c[N:P, :]).then_inc(gate_step, 1)
                wait_pairs(s, y_ready, i)
                for h in range(2):
                    cut, rows = slice(h * L, (h + 1) * L), slice(h * N, (h + 1) * N)
                    A(sp[rows, :], ex1[0:N, cut], ACT.Ln, bias=one_c[0:N, :])
                s.wait_ge(gate_step, 2 * i + 2)
                for h in range(2):
                    cut, rows = slice(h * L, (h + 1) * L), slice(h * N, (h + 1) * N)
                    last = A(qd[rows, :], ln_c[N:P, cut], ACT.Exp, scale=-1.0)
                last.then_inc(gates_ready, 1)

            def gate_attention(i):
                s.wait_ge(wo_done, i + 1)
                wait_pairs(s, tr2_done, i)
                modulate([att[:, h * L:(h + 1) * L] for h in range(2)], o_ps, i, mod[:, 2, :], ga_bo[:]).then_inc(att_ready, 1)

            def affine2(i):
                s.wait_ge(tr3_done, i + 1)
                wait_pairs(s, router_done, i)
                wait_pairs(s, split_done, i)
                modulate([h2[:, h * L:(h + 1) * L] for h in range(2)], t3_ps, i, mod[:, 4, :], mod[:, 3, :]).then_inc(h2_ready, 1)

            def softmax_exp(i):
                s.wait_ge(shifted, i + 1)
                A(exl[:], lgm[:], ACT.Exp).then_inc(exp_done, 1)

            def keep_scores(i):
                s.wait_ge(tr4_done, i + 1)
                A(pair_cols(scores, i, L), t4_ps[:, 0:L], ACT.Copy).then_inc(s_ready, 1)

            run_pairs(s, ((take_psum, 2), (affine1, 1), (gates, 2), (gate_attention, 3), (softmax_exp, 6),
                          (lambda i: rstd_guess(i, 1), 4), (lambda i: rstd_guess(i, 0), 0), (affine2, 5),
                          (keep_scores, 7)))

            def silu_pair(i):
                for k in range(CH):
                    g, q = i * CH + k, k // GROUP
                    s.wait_ge(up_done, g + 1)
                    if k % GROUP == 0:
                        wait_pairs(s, spilled[q % SLOTS], 16 * (i * (CH // GROUP // SLOTS) + q // SLOTS))
                    A(silu_ring[:, q % SLOTS, (k % GROUP) * PT:(k % GROUP + 1) * PT], bank[k % 4][:], ACT.Silu,
                      bias=bup_c[:, k:k + 1], scale=1.0 / W_SCALE).then_inc(silu_done, 1)

            silu_pair(0)
            with s.Fori(1, PAIRS) as i:
                silu_pair(i)

            def fs_high(i, par):
                s.wait_ge(fsn_ready, i + 1)
                dst = fs2[:, par * PT:(par + 1) * PT]
                A(dst[0:E, 0:L], fsn[0:E, :], ACT.Copy, scale=FS_SCALE)
                A(dst[0:E, L:PT], fsn[E:P, :], ACT.Copy, scale=FS_SCALE)
                A(fs_h1[E:P, :], fsn[E:P, :], ACT.Copy, scale=FS_SCALE).then_inc(fs_hi_ready, 1)

            def high_part(g, k):
                s.wait_ge(weighted, g + 1)
                wait_pairs(s, down_done, g + 1 - RING)
                A(act_hi[:, k % RING, :], act[:, k % 4, :], ACT.Copy).then_inc(hi_ready, 1)

            def gate_experts(i, par):
                s.wait_ge(out_done, i + 1)
                wait_pairs(s, tr5_done, i)
                for h in range(2):
                    last = A(oT[:, h * L:(h + 1) * L], bank[6 + par][:, h * L:(h + 1) * L], ACT.Copy,
                             scale=mod[:, 5, bass.ds(i + h * PAIRS, 1)])
                last.then_inc(o_ready, 1)

            def store(i):
                s.wait_ge(fin_ready, i + 1)
                for h in range(2):
                    s.dma_start(out_view[bass.ds(i, 1), h].rearrange("a p s d -> (a p) s d"),
                                pair_cols(xres, i)[:, h * L:(h + 1) * L].rearrange("p (s d) -> p s d", d=D)
                                ).then_inc(stored, 16)

            def experts(i, par, first=False, last=False):
                for k in range(CH):
                    high_part(i * CH + k, k)
                    if k == 3 and not first:
                        gate_experts(i - 1, 1 - par)
                    if k == 11 and not last:
                        fs_high(i + 1, 1 - par)
                    if k == 9 and not first:
                        store(i - 1)

            fs_high(0, 0)
            run_experts(s, experts)
            gate_experts(PAIRS - 1, 1)
            store(PAIRS - 1)
            s.wait_ge(stored, 32 * PAIRS)

        @block.tensor
        def _(pe):
            M = nc.tensor.matmul
            T = nc.tensor.transpose
            pe.wait_ge(params_in, N_PARAMS)
            pe.wait_ge(c_silu, 1)
            T(bank[0][:, 0:B], cs_sb[:], ident[0:B, 0:B]).then_inc(cT_done, 1)
            M(bank[2][:, 0:1], wp_sb[:], cols[:, 0:1], start=True, stop=True).then_inc(biasp_done, 1)
            pe.wait_ge(cT_copied, 1)
            for m in range(6):
                last = M(bank[1][:, m * B:(m + 1) * B], sort_c[:, m * D:(m + 1) * D], cT[:], start=True, stop=True)
            last.then_inc(mod_done, 1)
            pe.wait_ge(prep_done, 1)
            pe.wait_ge(zeroed, 5)

            def turn1(i):
                pe.wait_ge(xn_ready[0], i + 1)
                wait_pairs(pe, h_ready, i)
                for t in range(TILES):
                    last = T(t1_ps[:, t * P:(t + 1) * P], xn1[:, t, :], ident)
                last.then_inc(tr1_done, 1)

            def project(i):
                pe.wait_ge(h_ready, i + 1)
                wait_pairs(pe, psum_taken, i)
                M(u_ps[0:N, :].rearrange("p (h t) -> p h t", h=2), ws_sb[:], hT[:, :, PAD:ROW], start=True, stop=True)
                for k in range(TAPS):
                    last = M(proj_ps[:].rearrange("p (h t) -> p h t", h=2), wtap[:, k, :], hT[:, :, k:k + L],
                             start=(k == 0), stop=(k == TAPS - 1))
                last.then_inc(proj_done, 1)

            def attention_out(i):
                pe.wait_ge(y_ready, i + 1)
                wait_pairs(pe, att_ready, i)
                M(o_ps[:, 0:L], wo_a[:], y[:], start=True, stop=True)
                M(o_ps[:, L:PT], wo_b[:], y[:], start=True, stop=True).then_inc(wo_done, 1)

            def turn2(i):
                pe.wait_ge(att_ready, i + 1)
                wait_pairs(pe, resid_done, i)
                for t in range(TILES):
                    last = T(t2_ps[:, t * P:(t + 1) * P], att[:, t * P:(t + 1) * P], ident)
                last.then_inc(tr2_done, 1)

            def turn3(i):
                pe.wait_ge(xn_ready[1], i + 1)
                wait_pairs(pe, h2_ready, i)
                for t in range(TILES):
                    last = T(t3_ps[:, t * P:(t + 1) * P], xn2[:, t, :], ident)
                last.then_inc(tr3_done, 1)

            def router(i):
                pe.wait_ge(h2_ready, i + 1)
                wait_pairs(pe, shifted, i)
                for h in range(2):
                    for p in range(TILES // 2):
                        t, k = h * (TILES // 2) + p, p * 2 + h
                        last = M(lg_ps[:, k * E:(k + 1) * E], h2[:, t * P:(t + 1) * P], wr_sb[:], start=True, stop=True)
                last.then_inc(router_done, 1)

            def turn4(i):
                pe.wait_ge(sc_ready, i + 1)
                wait_pairs(pe, s_ready, i)
                for p in range(TILES // 2):
                    last = T(t4_ps[:, p * P:(p + 1) * P], sc[:, 2 * p:2 * p + 2, :].rearrange("p t e -> p (t e)"), ident)
                last.then_inc(tr4_done, 1)

            run_pairs(pe, ((turn1, 1), (attention_out, 3), (project, 1), (turn3, 5), (turn2, 3), (turn4, 7),
                           (router, 5)))

            def chunk_w(t, k):
                return t[:, k * P:(k + 1) * P]

            def three_products(dst, w_hi, w_lo, hi, lo):
                M(dst, w_hi, hi, start=True, stop=False)
                M(dst, w_hi, lo, start=False, stop=False)
                return M(dst, w_lo, hi, start=False, stop=True)

            def up_pair(i):
                pe.wait_ge(split_done, i + 1)
                hi, lo = pair_cols(h2_hi, i), pair_cols(h2_lo, i)
                for k in range(CH):
                    wait_pairs(pe, silu_done, i * CH + k - 3)
                    three_products(bank[k % 4][:], chunk_w(up_hi, k), chunk_w(up_lo, k), hi, lo).then_inc(up_done, 1)

            pe.wait_ge(wsplit_done, N_WEIGHTS)
            pe.wait_ge(h_ready, PAIRS)
            pe.wait_ge(psum_taken, PAIRS)
            pe.wait_ge(att_ready, PAIRS)
            up_pair(0)
            with pe.Fori(1, PAIRS) as i:
                up_pair(i)
            pe.wait_ge(silu_done, PAIRS * CH)

            ones = const("ones")
            with pe.Fori(0, DIGITS) as i:
                pe.wait_ge(cnt_ready, i + 1)
                M(bank[0][:, 0:DIGIT], ones, rc[:, 24:24 + DIGIT], start=True, stop=True).then_inc(cnt_summed, 1)
            pe.wait_ge(cnt_ready, DIGITS + 1)
            M(bank[0][:, 0:1], ones, rc[:, 24:25], start=True, stop=True).then_inc(cnt_summed, 1)
            pe.wait_ge(tie_ready, 1)
            M(bank[1][:, 0:NG], const("same_half"), gw[:, 2, :], start=True, stop=True)
            M(bank[2][:, 0:NG], const("before"), gw[:, 2, :], start=True, stop=True)
            M(bank[3][:, 0:1], ones, rc[:, 4:5], start=True, stop=True)
            M(bank[3][:, 1:2], const("from_half0"), rc[:, 5:6], start=True, stop=True).then_inc(tie_done, 1)
            pe.wait_ge(rsum_ready, 1)
            M(bank[4][:, 0:1], const("pair_sum"), rc[:, 13:14], start=True, stop=True).then_inc(rsum_done, 1)
            pe.wait_ge(rsum_ready, 2)
            M(bank[4][:, 2:3], const("pair_sum"), rc[:, 18:19], start=True, stop=True)
            M(bank[4][:, 3:4], const("shift_up"), rc[:, 19:20], start=True, stop=True).then_inc(rsum_done, 1)

            def denominators(i, par):
                pe.wait_ge(fsn_ready, i + 1)
                for p in range(TILES // 2):
                    last = M(bank[6 + par][:, 2 * p:2 * p + 2], fsn[:, p * P:(p + 1) * P], const("same_half")[:, 0:P:E],
                             start=True, stop=True)
                last.then_inc(den_done, 1)

            def down(i, k, par):
                g, acc, slot = i * CH + k, bank[6 + par], k % RING
                if k == 0:
                    pe.wait_ge(rden_ready, i + 1)
                    M(acc[:, 0:L], bd_a[:], fsn[:], start=True, stop=False, skip_group_check=True)
                    M(acc[:, L:PT], bd_b[:], fsn[:], start=False, stop=False, skip_group_check=True)
                pe.wait_ge(lo_ready, g + 1)
                M(acc[:], chunk_w(down_hi, k), act_hi[:, slot, :], start=False, stop=False, skip_group_check=True)
                M(acc[:], chunk_w(down_lo, k), act_hi[:, slot, :], start=False, stop=False, skip_group_check=True)
                M(acc[:], chunk_w(down_hi, k), act_lo[:, slot, :], start=False, stop=(k == CH - 1),
                  skip_group_check=True).then_inc(out_done if k == CH - 1 else down_done, 1)
                if k == CH - 1:
                    pe.wait_ge(out_done, i + 1)
                    pe.sem_inc(down_done, 1)

            def turn5(i, par):
                pe.wait_ge(o_ready, i + 1)
                for t in range(TILES):
                    last = T(bank[6 + par][:, t * P:(t + 1) * P], oT[:, t * P:(t + 1) * P], ident)
                last.then_inc(tr5_done, 1)

            LAG = 3

            def experts(i, par, first=False, last=False):
                hi, lo = pair_cols(h2_hi, i), pair_cols(h2_lo, i)
                for k in range(CH):
                    g = i * CH + k
                    wait_pairs(pe, gated, g - 3)
                    three_products(bank[k % 4][:], chunk_w(gate_hi, k), chunk_w(gate_lo, k), hi, lo).then_inc(gate_done, 1)
                    if k == 0:
                        pe.wait_ge(fs2_ready, i + 1)
                    wait_pairs(pe, weighted, g - 1)
                    M(bank[4 + k % 2][:], chunk_w(sel, k), fs2[:, par * PT:(par + 1) * PT],
                      start=True, stop=True).then_inc(fsb_done, 1)
                    if k >= LAG:
                        down(i, k - LAG, par)
                    elif not first:
                        down(i - 1, CH - LAG + k, 1 - par)
                    if k == 5 and not first:
                        turn5(i - 1, 1 - par)
                    if k == 12 and not last:
                        if not first:
                            pe.wait_ge(fin_ready, i)
                        denominators(i + 1, 1 - par)

            denominators(0, 0)
            run_experts(pe, experts)
            for k in range(CH - LAG, CH):
                down(PAIRS - 1, k, 1)
            turn5(PAIRS - 1, 1)


def shape_constants(np):
    p = np.arange(128)
    half, e = p // 64, p % 64
    src, dst = p[:, None], p[None, :]
    same = half[:, None] == half[None, :]
    blocks = [
        src == dst,
        np.ones((128, 128), bool),
        same,
        same & (src < dst),
        (half[:, None] == 0) & (half[None, :] == 1),
        dst == src + 64,
        e[:, None] == e[None, :],
        64 * half[:, None] + np.arange(64)[None, :],
    ]
    tail = np.zeros((128, 3), np.float32)
    tail[:, 0], tail[:, 1] = 1e-5, 1.0
    tail[:, 2] = 1.0 + half
    digit = np.broadcast_to((np.arange(1, 8, dtype=np.int32) << 28).view(np.float32), (128, 7))
    cst = np.concatenate([np.asarray(b, np.float32) for b in blocks] + [tail, digit], axis=1)
    chunk, a = np.arange(16), np.arange(128) // 32
    sel = e[:, None, None] == (4 * chunk[:, None] + a[None, :])[None]
    return cst.astype(np.float32), sel.reshape(128, 16 * 128).astype(np.float16)


def kernel(**inputs):
    import numpy as _np
    import concourse.bacc as _bacc
    from concourse import mybir as _mybir
    from concourse.bass_utils import run_bass_kernel_spmd as _run

    nc = _bacc.Bacc("TRN2", target_bir_lowering=False, num_devices=1)
    arrays, args = {}, []
    attn = {k[len("L0_attn_"):]: _np.asarray(v) for k, v in inputs.items() if k.startswith("L0_attn_")}
    ffn = {k[len("L0_ffn_"):]: _np.asarray(v) for k, v in inputs.items() if k.startswith("L0_ffn_")}
    E, D, H = ffn["Wup"].shape
    A = 128 // H

    def by_chunk(v):
        return v.reshape(E // A, A * H).T

    twice = [_np.concatenate([attn[n], attn[n]])[:, None] for n in ("bs", "A_log", "dt_log")]
    params = _np.concatenate([attn["conv_w"][:, 0].T] + [attn[n][:, None] for n in ("conv_b", "bp", "bo")] + twice
                             + [by_chunk(ffn["bup"]), by_chunk(ffn["bgate"])], axis=1)
    given = [("x", attn["x"]), ("Wp", attn["Wp"]), ("Ws", attn["Ws"]), ("Wo", attn["Wo"]), ("Wr", ffn["Wr"]),
             ("br", ffn["br"]),
             ("Wup", ffn["Wup"].transpose(1, 0, 2).reshape(D, E * H)),
             ("Wgate", ffn["Wgate"].transpose(1, 0, 2).reshape(D, E * H)),
             ("Wdown", ffn["Wdown"].reshape(E // A, A * H, D).transpose(1, 0, 2).reshape(A * H, E // A * D)),
             ("bdown", ffn["bdown"]), ("c", _np.asarray(inputs["L0_c"])), ("wmod", _np.asarray(inputs["L0_wmod"])),
             ("params", params)]
    cst, sel = shape_constants(_np)
    for name, a in given + [("consts", cst), ("selectors", sel)]:
        a = _np.ascontiguousarray(a)
        arrays[f"in_{name}"] = a
        args.append(nc.dram_tensor(f"in_{name}", a.shape, _mybir.dt.from_np(a.dtype), kind="ExternalInput").ap())
    args.append(nc.dram_tensor("out_x", (32, 256, 128), F32, kind="ExternalOutput").ap())
    adaln_kernel(nc, *args)
    r = _run(nc, [arrays], core_ids=[0])
    return r.results[0]["out_x"]
```

```python
from contextlib import ExitStack

import concourse.bass as bass
from concourse import mybir

F32 = mybir.dt.float32
F16 = mybir.dt.float16
I32 = mybir.dt.int32
ALU = mybir.AluOpType
ACT = mybir.ActivationFunctionType
AX = mybir.AxisListType

P = 128
CONSTS = ["ident", "ones", "same_half", "before", "from_half0", "shift_up", "pair_sum", "rank"]
CLAMP = 30.0
W_SCALE = 32.0
FS_SCALE = 4096.0


class Chain:

    def __init__(self, eng, sem, start=0):
        self.eng, self.sem, self.n = eng, sem, start

    def add(self, ins):
        ins.then_inc(self.sem, 1)
        self.n = self.n + 1

    def then_wait(self, ins):
        self.add(ins)
        self.eng.wait_ge(self.sem, self.n)


def wait_pairs(eng, sem, n):
    if not isinstance(n, int) or n > 0:
        eng.wait_ge(sem, n)


def adaln_kernel(nc, x, Wp, Ws, Wo, Wr, br, Wup, Wgate, Wdown, bdown, c, wmod, params, consts, sel_const, out):
    B, L, D = x.shape
    N = Ws.shape[1]
    E = Wr.shape[1]
    H = Wup.shape[1] // E
    TAPS = params.shape[1] - 6 - 2 * (E * H // P)
    PAIRS = B // 2
    PT = 2 * L
    TILES = PT // P
    HALF = PAIRS * L
    CH = E * H // P
    SLOTS, GROUP, RING = 4, 2, 8
    SPLIT_BY_DVE = [2, 12]
    DIGIT, DIGITS = 7, 10
    EC = P // H
    G = 64
    SPILLS_AHEAD = PAIRS - 1
    BUDGET = (B * L // G) * 16
    NG = HALF // G
    EPS = 1e-5
    PAD = TAPS - 1
    ROW = L + PAD

    with ExitStack() as ctx:
        def sb(name, shape, dt=F32):
            return ctx.enter_context(nc.sbuf_tensor(name, shape, dt))

        def sem(name):
            return ctx.enter_context(nc.semaphore(name))

        bank = [ctx.enter_context(nc.psum_tensor(f"bank{k}", [P, 512], F32)) for k in range(8)]

        xres = sb("xres", [P, PAIRS * PT])
        scores = sb("scores", [P, HALF])
        h2_hi = sb("h2_hi", [P, PAIRS * PT], F16)
        h2_lo = sb("h2_lo", [P, PAIRS * PT], F16)
        cst = sb("cst", [P, 7 * P + NG + 12])
        sel = sb("sel", [P, CH * P], F16)
        up_hi, up_lo = sb("up_hi", [P, CH * P], F16), sb("up_lo", [P, CH * P], F16)
        gate_hi, gate_lo = sb("gate_hi", [P, CH * P], F16), sb("gate_lo", [P, CH * P], F16)
        down_hi, down_lo = sb("down_hi", [P, CH * P], F16), sb("down_lo", [P, CH * P], F16)
        mod = sb("mod", [P, 6, B])
        ga_bo = sb("ga_bo", [P, B])
        sort_a, sort_b, sort_c = sb("sort_a", [P, HALF]), sb("sort_b", [P, HALF]), sb("sort_c", [P, HALF])
        wtap = sb("wtap", [P, TAPS, 2 * N])
        wp_sb, ws_sb = sb("wp_sb", [P, 2 * N]), sb("ws_sb", [P, N])
        wo_a, wo_b = sb("wo_a", [P, D]), sb("wo_b", [P, D])
        wr_sb = sb("wr_sb", [P, E])
        bd_a, bd_b = sb("bd_a", [P, D]), sb("bd_b", [P, D])
        br_row = sb("br_row", [P, E])
        par = sb("par", [P, TAPS + 6 + 2 * CH])
        conv_sb, cols = par[:, 0:TAPS], par[:, TAPS:TAPS + 3]
        ssm_in = par[:, TAPS + 3:TAPS + 6]
        bup_c, bgate_c = par[:, TAPS + 6:TAPS + 6 + CH], par[:, TAPS + 6 + CH:TAPS + 6 + 2 * CH]
        ssm = sb("ssm", [P, 24])
        c_sb, cs_sb, cT = sb("c_sb", [B, D]), sb("cs_sb", [B, D]), sb("cT", [P, B])
        tmp6 = sb("tmp6", [P, 3, 2 * B])
        bias_p = sb("bias_p", [P, 2])
        decay_row = sb("decay_row", [P, L])
        tick = sb("tick", [P, 2])
        stat, mv = sb("stat", [P, 2, TILES, 6]), sb("mv", [P, 2, TILES, 2])
        rstd = sb("rstd", [P, 2, 6, TILES])
        s1_buf = [sort_c[:, 6 * D + k * PT:6 * D + (k + 1) * PT] for k in range(6)]
        xn1, xn2 = (v.rearrange("p (t d) -> p t d", d=D) for v in s1_buf[0:2])
        hT = sb("hT", [P, 2, ROW])
        tcl, ex1, ln_c = s1_buf[2:5]
        s1_scan = sb("s1_scan", [P, 4 * PT])
        over, ub = s1_scan[:, 0:PT], s1_scan[:, PT:2 * PT]
        sp, qd, cd, spo = (s1_scan[:, 2 * PT + k * L:2 * PT + (k + 1) * L] for k in range(4))
        bu, state, y = sb("bu", [P, L]), sb("state", [P, L]), sb("y", [P, L])
        silu_up = s1_scan[:].rearrange("p (r t) -> p r t", r=4)
        att, h2 = s1_buf[5], sb("h2", [P, PT])
        lg, lgm, exl, sc = (sb(n, [P, TILES, E]) for n in ("lg", "lgm", "exl", "sc"))
        smx = sb("smx", [P, 3, TILES])
        gsum, gmin, gw = sb("gsum", [P, NG]), sb("gmin", [P, NG]), sb("gw", [P, 6, NG])
        bits = sb("bits", [P, 24], I32)
        ge = sort_c[:, 0:7 * NG].rearrange("p (d q) -> p d q", d=7)
        rc = sb("rc", [P, 44])
        act = sort_a[:].rearrange("p (r t) -> p r t", r=RING)
        act_hi, act_lo = (sort_b[:, k * 4 * PT:(k + 1) * 4 * PT].bitcast(F16).rearrange("p (r t) -> p r t", r=8)
                          for k in range(2))
        oT = sort_c[:, 0:PT]
        h_ring = sb("h_ring", [P, SLOTS, GROUP * PT])
        h_dram = nc.dram_tensor("gated_up", (PAIRS, CH // GROUP, P, GROUP * PT), F32, kind="Internal").ap()
        h_back = [h_ring[:, k, :] for k in range(SLOTS)]
        for t in (up_hi, up_lo, gate_hi, gate_lo, h2_hi, h2_lo):
            v = t[:].bitcast(F32)
            h_back += [v[:, k:k + GROUP * PT] for k in range(0, v.shape[1], GROUP * PT)]
        fs2 = sort_c[:, 4 * PT:5 * PT].bitcast(F16)
        fsn, eq, cum, kept = (sort_c[:, PT + k * L:PT + (k + 1) * L] for k in range(4))
        den, rden = sb("den", [P, TILES]), sb("rden", [P, 2 * TILES])
        fs_h1 = sort_c[:, 5 * PT:5 * PT + L // 2].bitcast(F16)

        def const(name):
            k = CONSTS.index(name)
            return cst[:, k * P:(k + 1) * P] if name != "rank" else cst[:, k * P:k * P + NG]
        eps_c = cst[:, 7 * P + NG:7 * P + NG + 1]
        one_c = cst[:, 7 * P + NG + 1:7 * P + NG + 2]
        expscale_c = cst[:, 7 * P + NG + 2:7 * P + NG + 3]
        topdigit_c = cst[:, 7 * P + NG + 3:7 * P + NG + 10]
        half_c, three_c = (cst[:, 7 * P + NG + 10 + k:7 * P + NG + 11 + k] for k in range(2))
        ident = const("ident")

        params_in, w_in, x_in = (sem(n) for n in ("params_in", "w_in", "x_in"))
        c_silu, cT_done, cT_copied, mod_done = (sem(n) for n in ("c_silu", "cT_done", "cT_copied", "mod_done"))
        biasp_done, setup_step, prep_done, ssm_step, ssm_done = (
            sem(n) for n in ("biasp_done", "setup_step", "prep_done", "ssm_step", "ssm_done"))
        zeroed, wsplit_done = sem("zeroed"), sem("wsplit_done")
        mv_ready, rs_step, rs_ready = ([sem(f"{n}{k}") for k in (1, 2)] for n in ("mv_ready", "rs_step", "rs_ready"))
        stat_step, norm_step, xn_ready = ([sem(f"{n}{k}") for k in (1, 2)] for n in ("stat_step", "norm_step", "xn_ready"))
        tr1_done, h_ready, proj_done, clamped, gate_step, gates_ready, psum_taken = (
            sem(n) for n in ("tr1_done", "h_ready", "proj_done", "clamped", "gate_step", "gates_ready", "psum_taken"))
        scan_step, y_ready, wo_done, att_ready, tr2_done, resid_done = (
            sem(n) for n in ("scan_step", "y_ready", "wo_done", "att_ready", "tr2_done", "resid_done"))
        tr3_done, h2_ready, split_step, split_done, router_done = (
            sem(n) for n in ("tr3_done", "h2_ready", "split_step", "split_done", "router_done"))
        sm_step, shifted, exp_done, sc_ready, tr4_done, s_ready = (
            sem(n) for n in ("sm_step", "shifted", "exp_done", "sc_ready", "tr4_done", "s_ready"))
        sort_step, route_step, cnt_ready, cnt_summed = (
            sem(n) for n in ("sort_step", "route_step", "cnt_ready", "cnt_summed"))
        swap_in = [sem(f"swap_in{k}") for k in range(2)]
        tie_ready, tie_done, rsum_ready, rsum_done, vswap_ready, vswap_in, fs_ready = (
            sem(n) for n in ("tie_ready", "tie_done", "rsum_ready", "rsum_done", "vswap_ready", "vswap_in", "fs_ready"))
        choose_step, rden_ready = sem("choose_step"), sem("rden_ready")
        den_done, den_step, fsn_ready, fs_hi_ready, fs2_ready = (
            sem(n) for n in ("den_done", "den_step", "fsn_ready", "fs_hi_ready", "fs2_ready"))
        spilled = [sem(f"spilled{k}") for k in range(SLOTS)]
        loaded = [sem(f"loaded{k}") for k in range(2 * CH // GROUP)]
        lg_step = sem("lg_step")
        c_in, first_in, w_high = sem("c_in"), sem("first_in"), sem("w_high")
        rstd_ready, spo_step, bu_ready = [sem(f"rstd_ready{k}") for k in (1, 2)], sem("spo_step"), sem("bu_ready")
        lo_dve, sorted_halves = sem("lo_dve"), sem("sorted_halves")
        gate_ready, gated_up = sem("gate_ready"), sem("gated_up")
        up_done, gate_done, fsb_done, silu_done, weighted, hi_ready, lo_ready, down_done = (
            sem(n) for n in ("up_done", "gate_done", "fsb_done", "silu_done", "weighted", "hi_ready",
                             "lo_ready", "down_done"))
        out_done, o_ready, tr5_done, fin_ready, stored = (
            sem(n) for n in ("out_done", "o_ready", "tr5_done", "fin_ready", "stored"))

        x_view = x.rearrange("(h j) (s p) d -> j h p s d", h=2, p=P)
        out_view = out.rearrange("(h j) (s p) d -> j h p s d", h=2, p=P)

        def pair_cols(t, i, w=PT):
            return t[:, bass.ds(i * w, w)]

        N_PARAMS = 16 * 8
        WEIGHT_PIECES = 6

        bufs = [sort_a, sort_b]

        def apart(t, j):
            v = t[:].rearrange("p (n a j) -> p n a j", a=2, j=j)
            return v[:, :, 0, :], v[:, :, 1, :]

        def within(t, k, first, end, j):
            v = t[:].rearrange("p (n k) -> p n k", k=k)[:, :, first:end].rearrange("p n (m a j) -> p n m a j", a=2, j=j)
            return v[:, :, :, 0, :], v[:, :, :, 1, :]

        log = HALF.bit_length() - 1
        STEPS = log * (log + 1) // 2
        sorted_in, merged_in = bufs[(STEPS - 1) % 2], bufs[STEPS % 2]

        DEEPEST = 7

        def run_pairs(eng, stages):
            def step(t):
                for stage, lag in stages:
                    if not isinstance(t, int) or 0 <= t - lag < PAIRS:
                        stage(t - lag)

            for t in range(DEEPEST + 1):
                step(t)
            with eng.Fori(DEEPEST + 1, PAIRS) as t:
                step(t)
            for t in range(PAIRS, PAIRS + DEEPEST):
                step(t)

        def run_experts(eng, experts):
            experts(0, 0, first=True)
            with eng.Fori(0, (PAIRS - 2) // 2) as j:
                experts(2 * j + 1, 1)
                experts(2 * j + 2, 0)
            experts(PAIRS - 1, 1, last=True)

        def wait_low(eng, i, k):
            if k in SPLIT_BY_DVE:
                eng.wait_ge(lo_dve, i * len(SPLIT_BY_DVE) + SPLIT_BY_DVE.index(k) + 1)
            else:
                by_pool = [c for c in range(CH) if c not in SPLIT_BY_DVE]
                eng.wait_ge(lo_ready, i * len(by_pool) + by_pool.index(k) + 1)

        def wait_slot_split(eng, i, k, first):
            if k >= RING:
                wait_low(eng, i, k - RING)
            elif not first:
                wait_low(eng, i - 1, k - RING + CH)

        def low_part(eng, ops, i, k, done):
            eng.wait_ge(hi_ready, i * CH + k + 1)
            wait_pairs(eng, down_done, i * CH + k + 1 - RING)
            ops.tensor_tensor(act_lo[:, k % RING, :], act[:, k % RING, :], act_hi[:, k % RING, :],
                              ALU.subtract).then_inc(done, 1)

        def weight_piece(i):
            raw = [(sort_a[:, 0:CH * P], up_hi, up_lo), (sort_a[:, CH * P:2 * CH * P], gate_hi, gate_lo),
                   (sort_b[:, 0:CH * P], down_hi, down_lo)]
            per = WEIGHT_PIECES // len(raw)
            width = CH * P // per
            return [t[:, i % per * width:(i % per + 1) * width] for t in raw[i // per]]

        block = ctx.enter_context(nc.Block())

        @block.sync
        def _(sp_eng):
            sp_eng.dma_start(c_sb[:], c).then_inc(c_in, 16)
            sp_eng.dma_start(cst[:], consts).then_inc(first_in, 16)
            sp_eng.dma_start(sort_c[:, 0:6 * D], wmod).then_inc(first_in, 16)
            sp_eng.dma_start(par[:], params).then_inc(first_in, 16)

            def load_pair(i):
                for h in range(2):
                    sp_eng.dma_start(pair_cols(xres, i)[:, h * L:(h + 1) * L].rearrange("p (s d) -> p s d", d=D),
                                     x_view[bass.ds(i, 1), h].rearrange("a p s d -> (a p) s d")).then_inc(x_in, 16)

            load_pair(0)
            with sp_eng.Fori(1, PAIRS) as i:
                sp_eng.wait_ge(x_in, 32 * i)
                load_pair(i)
            def spill(i):
                for q in range(CH // GROUP):
                    sp_eng.wait_ge(gated_up, i * CH + (q + 1) * GROUP)
                    sp_eng.dma_start(h_dram[bass.ds(i, 1), q].rearrange("a p n -> (a p) n"),
                                     h_ring[:, q % SLOTS, :]).then_inc(spilled[q % SLOTS], 16)

            with sp_eng.Fori(0, SPILLS_AHEAD) as i:
                spill(i)
            for piece in range(2):
                sp_eng.wait_ge(sorted_halves, piece + 1)
                cut = slice(piece * HALF // 2, (piece + 1) * HALF // 2)
                sp_eng.dma_start(sort_c[0:E, cut], sorted_in[E:P, cut]).then_inc(swap_in[piece], 16)
                sp_eng.dma_start(sort_c[E:P, cut], sorted_in[0:E, cut]).then_inc(swap_in[piece], 16)
            for i in range(SPILLS_AHEAD, PAIRS):
                spill(i)
            for q in range(SLOTS):
                sp_eng.wait_ge(spilled[q], 16 * PAIRS * CH // GROUP // SLOTS)

            def load_h(i, slot):
                q = slot % (CH // GROUP)
                sp_eng.dma_start(h_back[slot], h_dram[bass.ds(i, 1), q].rearrange("a p n -> (a p) n")
                                 ).then_inc(loaded[slot], 16)

            sp_eng.wait_ge(swap_in[0], 32)
            sp_eng.wait_ge(swap_in[1], 32)
            for slot in range(2 * CH // GROUP):
                load_h(slot // (CH // GROUP), slot)

            def refill(i, par):
                for q in range(CH // GROUP):
                    slot = par * (CH // GROUP) + q
                    sp_eng.wait_ge(weighted, (i - 2) * CH + (q + 1) * GROUP)
                    load_h(i, slot)

            with sp_eng.Fori(1, PAIRS // 2) as j:
                refill(2 * j, 0)
                refill(2 * j + 1, 1)

        t1_ps, proj_ps, u_ps, o_ps, t2_ps, t3_ps, lg_ps, t4_ps = bank

        @block.gpsimd
        def _(pool):
            zeros = Chain(pool, zeroed)
            for t in (wo_a[N:P, :], wo_b[0:N, :], bd_a[E:P, :], bd_b[0:E, :], hT[:]):
                zeros.then_wait(nc.gpsimd.memset(t, 0.0))
            def newton(i, which):
                r = rstd[:, which]
                pool.wait_ge(rs_ready[which], i + 1)
                steps = Chain(pool, norm_step[which], i * 5)
                guess, square, v, half, out_r = (r[:, k, :] for k in range(1, 6))
                steps.add(nc.gpsimd.tensor_tensor(square, guess, guess, ALU.mult))
                steps.add(nc.gpsimd.tensor_tensor(v, mv[:, which, :, 1], eps_c.to_broadcast([P, TILES]), ALU.add))
                steps.then_wait(nc.gpsimd.tensor_tensor(half, guess, half_c.to_broadcast([P, TILES]), ALU.mult))
                steps.then_wait(nc.gpsimd.tensor_tensor(square, square, v, ALU.mult))
                steps.then_wait(nc.gpsimd.tensor_tensor(square, square, three_c.to_broadcast([P, TILES]), ALU.add))
                nc.gpsimd.tensor_tensor(out_r, square, half, ALU.mult).then_inc(rstd_ready[which], 1)

            def scan_input(i):
                pool.wait_ge(gates_ready, i + 1)
                nc.gpsimd.tensor_tensor(spo[:], sp[:], pair_cols(over, i % 2, L), ALU.add).then_inc(spo_step, 1)
                pool.wait_ge(spo_step, i + 1)
                nc.gpsimd.tensor_tensor(bu[:], spo[:], pair_cols(ub, i % 2, L), ALU.mult).then_inc(bu_ready, 1)

            def split(i):
                pool.wait_ge(h2_ready, i + 1)
                nc.gpsimd.tensor_copy(pair_cols(h2_hi, i), h2[:]).then_inc(split_step, 1)
                pool.wait_ge(split_step, i + 1)
                nc.gpsimd.tensor_tensor(pair_cols(h2_lo, i), h2[:], pair_cols(h2_hi, i),
                                        ALU.subtract).then_inc(split_done, 1)

            run_pairs(pool, ((lambda i: newton(i, 0), 1), (scan_input, 3), (lambda i: newton(i, 1), 5), (split, 6)))

            def gate_up(i):
                for k in range(CH):
                    g, q = i * CH + k, k // GROUP
                    pool.wait_ge(silu_done, g + 1)
                    pool.wait_ge(gate_ready, g + 1)
                    h = h_ring[:, q % SLOTS, (k % GROUP) * PT:(k % GROUP + 1) * PT]
                    nc.gpsimd.tensor_tensor(h, h, silu_up[:, k % 4, :], ALU.mult).then_inc(gated_up, 1)

            gate_up(0)
            with pool.Fori(1, PAIRS) as i:
                gate_up(i)

            def experts(i, par, first=False, last=False):
                for k in range(CH):
                    if k not in SPLIT_BY_DVE:
                        low_part(pool, nc.gpsimd, i, k, lo_ready)

            run_experts(pool, experts)

        @block.vector
        def _(dve):
            V = nc.vector
            setup = Chain(dve, setup_step)
            dve.wait_ge(first_in, 48)
            V.tensor_scalar(ssm[:, 4:6], ssm_in[:, 1:3], CLAMP, None, ALU.min).then_inc(ssm_step, 1)
            setup.add(V.tensor_scalar(ssm[:, 6:8], ssm_in[:, 1:3], CLAMP, 0.0, ALU.subtract, ALU.max))
            setup.add(V.memset(decay_row[:], 0.0))
            dve.wait_ge(cT_done, 1)
            V.tensor_copy(cT[:], bank[0][:, 0:B]).then_inc(cT_copied, 1)
            dve.wait_ge(ssm_done, 2)
            dve.wait_ge(setup_step, setup.n)
            setup.then_wait(V.tensor_tensor(ssm[:, 12:14], ssm[:, 6:8], ssm[:, 10:12], ALU.add))
            setup.add(V.tensor_tensor(ssm[:, 16:17], ssm_in[:, 0:1], ssm[:, 13:14], ALU.mult))
            setup.then_wait(V.tensor_tensor(ssm[:, 14:15], ssm[:, 12:13], ssm[:, 13:14], ALU.mult))
            setup.then_wait(V.tensor_scalar(ssm[:, 15:16], ssm[:, 14:15], -1.0, 1.0, ALU.mult, ALU.add))
            setup.add(V.tensor_scalar(decay_row[:], decay_row[:], ssm[:, 15:16], None, ALU.add))
            dve.wait_ge(params_in, N_PARAMS)
            for k in range(TAPS):
                setup.add(V.tensor_scalar(wtap[:, k, :], wp_sb[:], conv_sb[:, k:k + 1], None, ALU.mult))
            dve.wait_ge(zeroed, 5)
            setup.add(V.tensor_scalar(bd_a[:], bd_a[:], W_SCALE, None, ALU.mult))
            setup.add(V.tensor_scalar(bd_b[:], bd_b[:], W_SCALE, None, ALU.mult))
            dve.wait_ge(mod_done, 1)
            setup.then_wait(V.tensor_copy(mod[:], bank[1][:, 0:6 * B].rearrange("p (m b) -> p m b", b=B)))
            gains, scales = mod[:, 2:6:3, :], mod[:, 1:5:3, :]
            mag, sign = (tmp6[:, k, :].rearrange("p (m b) -> p m b", b=B) for k in range(2))
            setup.add(V.tensor_scalar(sign, gains, 0.0, 2.0, ALU.is_ge, ALU.mult))
            setup.then_wait(V.scalar_tensor_tensor(mag, gains, -1.0, gains, ALU.mult, ALU.max))
            setup.add(V.tensor_scalar(mag, mag, 0.25, None, ALU.max))
            setup.then_wait(V.tensor_scalar(scales, scales, 1.0, None, ALU.add))
            setup.then_wait(V.scalar_tensor_tensor(gains, sign, -1.0, mag, ALU.add, ALU.mult))
            setup.add(V.tensor_scalar(ga_bo[:], mod[:, 2, :], cols[:, 2:3], None, ALU.mult))
            setup.add(V.tensor_scalar(mod[:, 5, :], mod[:, 5, :], 1.0 / W_SCALE, None, ALU.mult))
            dve.wait_ge(biasp_done, 1)
            setup.then_wait(V.tensor_tensor(bias_p[:, 0:1], bank[2][:, 0:1], cols[:, 1:2], ALU.add))
            V.tensor_scalar(bias_p[:, 1:2], bias_p[:, 0:1], CLAMP, None, ALU.subtract).then_inc(prep_done, 1)

            def token_sums(i, which):
                if which == 0:
                    dve.wait_ge(x_in, 32 * i + 32)
                else:
                    dve.wait_ge(resid_done, i + 1)
                v = pair_cols(xres, i).rearrange("p (t d) -> p t d", d=D)
                V.memset(tick[:, 0:1], 0.0)
                for t in range(TILES):
                    V.bn_stats(stat[:, which, t, :], v[:, t, :]).then_inc(stat_step[which], 1)

            def token_stats(i, which):
                dve.wait_ge(stat_step[which], (i + 1) * TILES)
                V.memset(tick[:, 1:2], 0.0)
                for t in range(TILES):
                    last = V.bn_aggr(mv[:, which, t, :], stat[:, which, t, :])
                last.then_inc(mv_ready[which], 1)

            def norm(i, which, xn, xn_read):
                v = pair_cols(xres, i).rearrange("p (t d) -> p t d", d=D)
                r = rstd[:, which]
                dve.wait_ge(rstd_ready[which], i + 1)
                wait_pairs(dve, xn_read, i)
                for t in range(TILES):
                    last = V.tensor_scalar(xn[:, t, :], v[:, t, :], mv[:, which, t, 0:1], r[:, 5, t:t + 1],
                                           ALU.subtract, ALU.mult)
                last.then_inc(xn_ready[which], 1)

            def low_weights(i):
                if isinstance(i, int) and i < WEIGHT_PIECES:
                    w, hi, lo = weight_piece(i)
                    dve.wait_ge(w_high, i + 1)
                    V.scalar_tensor_tensor(lo, w, W_SCALE, hi, ALU.mult, ALU.subtract).then_inc(wsplit_done, 1)

            def clamp(i):
                dve.wait_ge(proj_done, i + 1)
                wait_pairs(dve, gate_step, 2 * i - 1)
                V.tensor_scalar(tcl[:], proj_ps[:], bias_p[:, 0:1], CLAMP, ALU.add, ALU.min).then_inc(clamped, 1)

            def scan(i):
                dve.wait_ge(gates_ready, i + 1)
                V.tensor_scalar(cd[:], qd[:], -2.0, 1.0, ALU.mult, ALU.add).then_inc(scan_step, 1)
                dve.wait_ge(bu_ready, i + 1)
                V.tensor_tensor_scan(state[:], decay_row[:], bu[:], 0.0, ALU.mult, ALU.add).then_inc(scan_step, 1)

            def scan_output(i):
                dve.wait_ge(scan_step, 2 * i + 2)
                wait_pairs(dve, wo_done, i)
                V.tensor_tensor(y[:], cd[:], state[:], ALU.mult).then_inc(y_ready, 1)

            def residual(i):
                dve.wait_ge(tr2_done, i + 1)
                V.tensor_tensor(pair_cols(xres, i), t2_ps[:], pair_cols(xres, i), ALU.add).then_inc(resid_done, 1)

            def logits(i):
                dve.wait_ge(router_done, i + 1)
                V.tensor_tensor(lg[:], lg_ps[:, 0:TILES * E].rearrange("p (t e) -> p t e", e=E),
                                br_row[:].unsqueeze(1).to_broadcast([P, TILES, E]), ALU.add).then_inc(lg_step, 1)

            def logits_max(i):
                dve.wait_ge(lg_step, 2 * i + 1)
                V.tensor_reduce(smx[:, 0, :], lg[:], AX.X, ALU.max).then_inc(lg_step, 1)

            def logits_less_max(i):
                dve.wait_ge(lg_step, 2 * i + 2)
                V.tensor_tensor(lgm[:], lg[:], smx[:, 0, :].unsqueeze(2).to_broadcast([P, TILES, E]),
                                ALU.subtract).then_inc(shifted, 1)

            def softmax_sum(i):
                dve.wait_ge(exp_done, i + 1)
                V.tensor_reduce(smx[:, 1, :], exl[:], AX.X, ALU.add).then_inc(sm_step, 1)

            def softmax_scale(i):
                dve.wait_ge(sm_step, 2 * i + 1)
                V.reciprocal(smx[:, 2, :], smx[:, 1, :]).then_inc(sm_step, 1)

            def softmax(i):
                dve.wait_ge(sm_step, 2 * i + 2)
                wait_pairs(dve, tr4_done, i)
                V.tensor_tensor(sc[:], exl[:], smx[:, 2, :].unsqueeze(2).to_broadcast([P, TILES, E]),
                                ALU.mult).then_inc(sc_ready, 1)

            run_pairs(dve, (
                (lambda i: norm(i, 0, xn1, tr1_done), 1), (clamp, 2), (scan, 3), (lambda i: token_sums(i, 0), 0),
                (scan_output, 3), (lambda i: token_stats(i, 0), 0), (low_weights, 2),
                (lambda i: norm(i, 1, xn2, tr3_done), 5), (residual, 4), (softmax_sum, 7),
                (lambda i: token_sums(i, 1), 4), (softmax_scale, 7), (logits, 6), (lambda i: token_stats(i, 1), 4),
                (logits_max, 6), (softmax, 7), (logits_less_max, 6)))

            dve.wait_ge(s_ready, PAIRS)
            dve.wait_ge(wsplit_done, WEIGHT_PIECES)
            order = Chain(dve, sort_step)

            def exchange(pair_of, src, dst, *where):
                a, b = pair_of(src, *where)
                oa, ob = pair_of(dst, *where)
                order.add(V.tensor_tensor(oa, a, b, ALU.max))
                order.add(V.tensor_tensor(ob, a, b, ALU.min))
                dve.wait_ge(sort_step, order.n)

            def exchange_split(src, dst, k, j):
                a0, b0 = within(dst, k, j, 3 * j, j)[0], within(src, k, j, 3 * j, j)[1]
                a1, b1 = within(src, k, k - 3 * j, k - j, j)[0], within(dst, k, k - 3 * j, k - j, j)[1]
                order.add(V.tensor_tensor(within(dst, k, j, 3 * j, j)[1], a0, b0, ALU.min))
                order.add(V.tensor_tensor(within(dst, k, k - 3 * j, k - j, j)[0], a1, b1, ALU.max))
                outer = order.n
                a, b = within(src, k, 3 * j, k - 3 * j, j)
                oa, ob = within(dst, k, 3 * j, k - 3 * j, j)
                order.add(V.tensor_tensor(oa, a, b, ALU.max))
                order.add(V.tensor_tensor(ob, a, b, ALU.min))
                dve.wait_ge(sort_step, outer)
                order.add(V.tensor_tensor(a0, a0, b0, ALU.max))
                order.add(V.tensor_tensor(b1, a1, b1, ALU.min))
                dve.wait_ge(sort_step, order.n)

            src, dst = scores, bufs[0]
            k = 2
            while k <= HALF:
                exchange(apart, src, dst, k // 2)
                home = dst
                src, dst = dst, bufs[1] if dst is bufs[0] else bufs[0]
                j = k // 4
                while j >= 1:
                    if j == 1 and dst is not home:
                        ends = [t[:].rearrange("p (n k) -> p n k", k=k)[:, :, 0:k:k - 1] for t in (dst, home)]
                        order.add(V.tensor_copy(*ends))
                    if k == HALF and j == 1:
                        break
                    if dst is home:
                        exchange_split(src, dst, k, j)
                    else:
                        exchange(within, src, dst, k, j, k - j, j)
                    src, dst = dst, src
                    j //= 2
                k *= 2
            def within_cols(t, first, end):
                return apart(t[:, first:end], 1)

            exchange(within_cols, src, dst, 1, HALF // 2 + 1)
            dve.sem_inc(sorted_halves, 1)
            exchange(within_cols, src, dst, HALF // 2 + 1, HALF - 1)
            dve.sem_inc(sorted_halves, 1)
            src, dst = dst, src
            for piece in range(2):
                dve.wait_ge(swap_in[piece], 32)
                cut = slice(HALF // 2, HALF) if piece == 0 else slice(0, HALF // 2)
                theirs = sort_c[:, HALF // 2 - 1::-1] if piece == 0 else sort_c[:, HALF - 1:HALF // 2 - 1:-1]
                order.add(V.tensor_tensor(merged_in[0:E, cut], src[0:E, cut], theirs[0:E], ALU.max))
                order.add(V.tensor_tensor(merged_in[E:P, cut], src[E:P, cut], theirs[E:P], ALU.min))
            dve.wait_ge(sort_step, order.n)
            src, dst = merged_in, src
            j = HALF // 2
            while j >= G:
                exchange(apart, src, dst, j)
                src, dst = dst, src
                j //= 2
            blocks = src[:].rearrange("p (q g) -> p q g", g=G)
            work = dst
            route = Chain(dve, route_step)
            route.add(V.tensor_reduce(gsum[:], blocks, AX.X, ALU.add))
            route.then_wait(V.tensor_reduce(gmin[:], blocks, AX.X, ALU.min))

            cur, bit, inc = (bits[:, k:k + 1] for k in range(3))
            digit_bits, trials = bits[:, 8:8 + DIGIT], bits[:, 16:16 + DIGIT]
            route.then_wait(V.memset(cur, 0))
            route.then_wait(V.tensor_copy(digit_bits, topdigit_c.bitcast(I32)))

            def search(i, n_trials, shift):
                tr, db = trials[:, 0:n_trials], digit_bits[:, 0:n_trials]
                route.then_wait(V.tensor_tensor(tr, db, cur.to_broadcast([P, n_trials]), ALU.bitwise_or))
                route.then_wait(V.tensor_tensor(ge[:, 0:n_trials, :], gsum[:].unsqueeze(1).to_broadcast([P, n_trials, NG]),
                                                tr.bitcast(F32).unsqueeze(2).to_broadcast([P, n_trials, NG]), ALU.is_ge))
                V.tensor_reduce(rc[:, 24:24 + n_trials], ge[:, 0:n_trials, :], AX.X, ALU.add).then_inc(cnt_ready, 1)
                dve.wait_ge(cnt_summed, i + 1)
                route.add(V.tensor_scalar(rc[:, 32:32 + n_trials], bank[0][:, 0:n_trials], float(BUDGET) - 0.5, None,
                                          ALU.is_ge, ALU.add, accum_out=rc[:, 40:41]))
                dve.wait_ge(route_step, route.n)
                route.then_wait(V.tensor_tensor(inc, rc[:, 40:41], digit_bits[:, 0:1], ALU.mult))
                route.then_wait(V.tensor_tensor(cur, cur, inc, ALU.bitwise_or))
                route.then_wait(V.tensor_scalar(digit_bits, digit_bits, shift, None, ALU.logical_shift_right))

            base = route.n
            PER = 6
            with dve.Fori(0, DIGITS) as i:
                route.n = base + i * PER
                search(i, DIGIT, 3)
            route.n = base + DIGITS * PER
            route.then_wait(V.memset(digit_bits, 1))
            search(DIGITS, 1, 0)
            theta = cur.bitcast(F32)

            above, equal = gw[:, 1, :], gw[:, 2, :]
            route.then_wait(V.tensor_scalar(above, gsum[:], theta, None, ALU.is_gt, ALU.add, accum_out=rc[:, 2:3]))
            route.then_wait(V.tensor_scalar(equal, gsum[:], theta, None, ALU.is_equal, ALU.add, accum_out=rc[:, 3:4]))
            V.tensor_copy(rc[:, 4:6], rc[:, 2:4]).then_inc(tie_ready, 1)
            dve.wait_ge(tie_done, 1)
            route.then_wait(V.tensor_copy(gw[:, 3, :], bank[1][:, 0:NG]))
            route.then_wait(V.tensor_tensor_scan(gw[:, 4, :], const("ones")[:, 0:NG], gw[:, 3, :], 0.0, ALU.mult, ALU.add))
            route.then_wait(V.tensor_tensor(gw[:, 4, :], gw[:, 4, :], gw[:, 3, :], ALU.subtract))
            route.then_wait(V.tensor_tensor(gw[:, 4, :], gw[:, 4, :], bank[2][:, 0:NG], ALU.add))
            route.then_wait(V.tensor_copy(rc[:, 6:8], bank[3][:, 0:2]))
            route.then_wait(V.tensor_tensor(rc[:, 12:13], rc[:, 6:7], rc[:, 7:8], ALU.add))
            route.then_wait(V.tensor_scalar(rc[:, 12:13], rc[:, 12:13], -1.0, float(BUDGET), ALU.mult, ALU.add))
            route.then_wait(V.scalar_tensor_tensor(gw[:, 5, :], gw[:, 4, :], rc[:, 12:13], equal, ALU.is_lt, ALU.mult))
            route.then_wait(V.tensor_tensor(gw[:, 5, :], gw[:, 5, :], above, ALU.add))
            V.tensor_reduce(rc[:, 13:14], gw[:, 5, :], AX.X, ALU.add).then_inc(rsum_ready, 1)
            dve.wait_ge(rsum_done, 1)
            route.then_wait(V.tensor_copy(rc[:, 14:15], bank[4][:, 0:1]))
            route.then_wait(V.tensor_scalar(gw[:, 0, :], const("rank"), rc[:, 14:15], 2.0, ALU.is_ge, ALU.mult))
            route.then_wait(V.tensor_tensor(gw[:, 0, :], gw[:, 0, :], gmin[:], ALU.max))
            V.tensor_reduce(rc[:, 8:9], gw[:, 0, :], AX.X, ALU.min).then_inc(vswap_ready, 1)
            dve.wait_ge(vswap_in, 32)
            route.then_wait(V.tensor_tensor(rc[:, 10:11], rc[:, 8:9], rc[:, 9:10], ALU.min))
            thr = rc[:, 10:11]
            route.add(V.tensor_scalar(work[:], scores[:], thr, None, ALU.is_gt, ALU.add, accum_out=rc[:, 16:17]))
            route.add(V.tensor_scalar(src[:], scores[:], thr, None, ALU.is_equal, ALU.add, accum_out=rc[:, 17:18]))
            dve.wait_ge(route_step, route.n)
            V.tensor_copy(rc[:, 18:20], rc[:, 16:18]).then_inc(rsum_ready, 1)
            dve.wait_ge(rsum_done, 2)
            route.then_wait(V.tensor_copy(rc[:, 20:22], bank[4][:, 2:4]))
            V.tensor_scalar(rc[:, 22:23], rc[:, 14:15], float(G), rc[:, 20:21], ALU.mult,
                            ALU.subtract).then_inc(fs_ready, 1)
            dve.wait_ge(fs_ready, 1)
            ties_seen, ties_wanted = rc[:, 21:22], rc[:, 22:23]

            def choose(i, part):
                s_i = pair_cols(scores, i, L)
                if part > 0:
                    dve.wait_ge(choose_step, i * 5 + part)
                if part == 0:
                    V.tensor_scalar(eq[:], s_i, thr, None, ALU.is_equal).then_inc(choose_step, 1)
                elif part == 1:
                    V.tensor_tensor_scan(cum[:], const("ones")[:, 0:1].to_broadcast([P, L]), eq[:], ties_seen,
                                         ALU.mult, ALU.add).then_inc(choose_step, 1)
                elif part == 2:
                    V.tensor_copy(ties_seen, cum[:, L - 1:L]).then_inc(choose_step, 1)
                elif part == 3:
                    V.scalar_tensor_tensor(eq[:], cum[:], ties_wanted, eq[:], ALU.is_le, ALU.mult).then_inc(choose_step, 1)
                elif part == 4:
                    V.scalar_tensor_tensor(kept[:], s_i, thr, eq[:], ALU.is_gt, ALU.add).then_inc(choose_step, 1)
                else:
                    if not isinstance(i, int) or i > 0:
                        dve.wait_ge(down_done, (i - 1) * CH + 1)
                    V.tensor_tensor(fsn[:], kept[:], s_i, ALU.mult).then_inc(fsn_ready, 1)

            def denominator(i, par):
                dve.wait_ge(den_done, i + 1)
                r = rden[:, par * TILES:(par + 1) * TILES]
                V.tensor_scalar(den[:], bank[6 + par][:, 0:TILES], 1e-6, None, ALU.add).then_inc(den_step, 1)
                dve.wait_ge(den_step, i + 1)
                V.reciprocal(r, den[:]).then_inc(rden_ready, 1)

            def fs_low(i, par):
                dve.wait_ge(fs_hi_ready, i + 1)
                dve.wait_ge(fsn_ready, i + 1)
                dst = fs2[:, par * PT:(par + 1) * PT]
                V.scalar_tensor_tensor(dst[E:P, 0:L], fsn[0:E, :], FS_SCALE, dst[0:E, 0:L], ALU.mult, ALU.subtract)
                V.scalar_tensor_tensor(dst[E:P, L:PT], fsn[E:P, :], FS_SCALE, fs_h1[E:P, :], ALU.mult,
                                       ALU.subtract).then_inc(fs2_ready, 1)

            def finish(i, par, tiles):
                dve.wait_ge(tr5_done, i + 1)
                dve.wait_ge(rden_ready, i + 1)
                v, r = pair_cols(xres, i), rden[:, par * TILES:(par + 1) * TILES]
                for t in tiles:
                    h, p = t // 2, t % 2
                    cut = slice(t * P, (t + 1) * P)
                    last = V.scalar_tensor_tensor(v[:, cut], bank[6 + par][:, cut], r[:, 2 * p + h:2 * p + h + 1], v[:, cut],
                                                  ALU.mult, ALU.add)
                if TILES - 1 in tiles:
                    last.then_inc(fin_ready, 1)

            def experts(i, par, first=False, last=False):
                for k in range(CH):
                    g = i * CH + k
                    slot = par * (CH // GROUP) + k // GROUP
                    if k % GROUP == 0:
                        dve.wait_ge(loaded[slot], 8 * (i - par) + 16)
                    dve.wait_ge(fsb_done, g + 1)
                    wait_slot_split(dve, i, k, first)
                    V.scalar_tensor_tensor(act[:, k % RING, :], bank[k % 4][:], 1.0 / FS_SCALE,
                                           h_back[slot][:, (k % GROUP) * PT:(k % GROUP + 1) * PT],
                                           ALU.mult, ALU.mult).then_inc(weighted, 1)
                    if k - 2 in SPLIT_BY_DVE:
                        low_part(dve, V, i, k - 2, lo_dve)
                    if 3 <= k <= 8 and not last:
                        choose(i + 1, k - 3)
                    if k in (9, 10) and not first:
                        finish(i - 1, 1 - par, range(2 * (k - 9), 2 * (k - 9) + 2))
                    if k == 13 and not last:
                        denominator(i + 1, 1 - par)
                    if k == 11 and not last:
                        fs_low(i + 1, 1 - par)

            for part in range(6):
                choose(0, part)
            fs_low(0, 0)
            denominator(0, 0)
            run_experts(dve, experts)
            finish(PAIRS - 1, 1, range(TILES))

        @block.scalar
        def _(s):
            A = nc.scalar.activation
            def load(dst, src):
                s.dma_start(dst, src).then_inc(params_in, 16)

            load(wp_sb[:], Wp)
            load(ws_sb[:], Ws)
            s.wait_ge(c_in, 16)
            A(cs_sb[:], c_sb[:], ACT.Silu).then_inc(c_silu, 1)
            load(bd_a[0:E, :], bdown)
            load(bd_b[E:P, :], bdown)
            load(wo_a[0:N, :], Wo)
            load(wo_b[N:P, :], Wo)
            load(wr_sb[:], Wr)
            load(br_row[:], br.partition_broadcast(P))
            s.wait_ge(first_in, 48)
            s.preload_act_table_set("natural_log_exp_and_others")
            s.wait_ge(ssm_step, 1)
            A(ssm[:, 8:10], ssm[:, 4:6], ACT.Exp).then_inc(ssm_done, 1)
            s.wait_ge(ssm_done, 1)
            A(ssm[:, 10:12], ssm[:, 8:10], ACT.Ln, bias=one_c).then_inc(ssm_done, 1)
            s.dma_start(sort_a[:, 0:2048], Wup).then_inc(w_in, 16)
            s.dma_start(sort_a[:, 2048:4096], Wgate).then_inc(w_in, 16)
            s.dma_start(sort_b[:, 0:2048], Wdown).then_inc(w_in, 16)
            s.dma_start(sel[:], sel_const).then_inc(w_in, 16)
            s.wait_ge(prep_done, 1)

            def high_weights(i):
                if isinstance(i, int) and i < WEIGHT_PIECES:
                    w, hi, lo = weight_piece(i)
                    if i == 0:
                        s.wait_ge(w_in, 64)
                    A(hi, w, ACT.Copy, scale=W_SCALE).then_inc(w_high, 1)

            def rstd_guess(i, which):
                s.wait_ge(mv_ready[which], i + 1)
                A(rstd[:, which, 0, :], mv[:, which, :, 1], ACT.Ln, bias=eps_c).then_inc(rs_step[which], 1)
                s.wait_ge(rs_step[which], i + 1)
                A(rstd[:, which, 1, :], rstd[:, which, 0, :], ACT.Exp, scale=-0.5).then_inc(rs_ready[which], 1)

            def modulate(dst, src, i, m_scale, m_shift):
                for h in range(2):
                    b = bass.ds(i + h * PAIRS, 1)
                    last = A(dst[h], src[:, h * L:(h + 1) * L], ACT.Identity, bias=m_shift[:, b], scale=m_scale[:, b])
                return last

            def affine1(i):
                s.wait_ge(tr1_done, i + 1)
                wait_pairs(s, proj_done, i)
                modulate([hT[:, h, PAD:ROW] for h in range(2)], t1_ps, i, mod[:, 1, :], mod[:, 0, :]).then_inc(h_ready, 1)

            def take_psum(i):
                s.wait_ge(proj_done, i + 1)
                wait_pairs(s, y_ready, i - 1)
                for h in range(2):
                    cut, rows = slice(h * L, (h + 1) * L), slice(h * N, (h + 1) * N)
                    A(pair_cols(ub, i % 2, L)[rows, :], u_ps[0:N, cut], ACT.Identity, bias=ssm[0:N, 16:17],
                      scale=ssm[0:N, 13:14])
                s.wait_ge(clamped, i + 1)
                for h in range(2):
                    cut, rows = slice(h * L, (h + 1) * L), slice(h * N, (h + 1) * N)
                    last = A(pair_cols(over, i % 2, L)[rows, :], proj_ps[0:N, cut], ACT.Relu, bias=bias_p[0:N, 1:2])
                last.then_inc(psum_taken, 1)

            def gates(i):
                A(ex1[:], tcl[:], ACT.Exp, scale=expscale_c).then_inc(gate_step, 1)
                s.wait_ge(gate_step, 2 * i + 1)
                A(ln_c[N:P, :], ex1[N:P, :], ACT.Ln, bias=one_c[N:P, :]).then_inc(gate_step, 1)
                wait_pairs(s, y_ready, i)
                for h in range(2):
                    cut, rows = slice(h * L, (h + 1) * L), slice(h * N, (h + 1) * N)
                    A(sp[rows, :], ex1[0:N, cut], ACT.Ln, bias=one_c[0:N, :])
                s.wait_ge(gate_step, 2 * i + 2)
                for h in range(2):
                    cut, rows = slice(h * L, (h + 1) * L), slice(h * N, (h + 1) * N)
                    last = A(qd[rows, :], ln_c[N:P, cut], ACT.Exp, scale=-1.0)
                last.then_inc(gates_ready, 1)

            def gate_attention(i):
                s.wait_ge(wo_done, i + 1)
                wait_pairs(s, tr2_done, i)
                modulate([att[:, h * L:(h + 1) * L] for h in range(2)], o_ps, i, mod[:, 2, :],
                         ga_bo[:]).then_inc(att_ready, 1)

            def affine2(i):
                s.wait_ge(tr3_done, i + 1)
                wait_pairs(s, router_done, i)
                wait_pairs(s, split_done, i)
                modulate([h2[:, h * L:(h + 1) * L] for h in range(2)], t3_ps, i, mod[:, 4, :],
                         mod[:, 3, :]).then_inc(h2_ready, 1)

            def softmax_exp(i):
                s.wait_ge(shifted, i + 1)
                A(exl[:], lgm[:], ACT.Exp).then_inc(exp_done, 1)

            def keep_scores(i):
                s.wait_ge(tr4_done, i + 1)
                A(pair_cols(scores, i, L), t4_ps[:, 0:L], ACT.Copy).then_inc(s_ready, 1)

            run_pairs(s, ((take_psum, 2), (affine1, 1), (gates, 2), (lambda i: rstd_guess(i, 0), 0), (gate_attention, 3),
                          (softmax_exp, 6), (lambda i: rstd_guess(i, 1), 4), (affine2, 5), (keep_scores, 7),
                          (high_weights, 1)))

            def up_and_gate(i):
                for k in range(CH):
                    g, q = i * CH + k, k // GROUP
                    s.wait_ge(up_done, g + 1)
                    wait_pairs(s, gated_up, g - 3)
                    A(silu_up[:, k % 4, :], bank[k % 4][:], ACT.Silu, bias=bup_c[:, k:k + 1],
                      scale=1.0 / W_SCALE).then_inc(silu_done, 1)
                    s.wait_ge(gate_done, g + 1)
                    if k % GROUP == 0:
                        wait_pairs(s, spilled[q % SLOTS], 16 * (i * (CH // GROUP // SLOTS) + q // SLOTS))
                    A(h_ring[:, q % SLOTS, (k % GROUP) * PT:(k % GROUP + 1) * PT], bank[4 + k % 4][:], ACT.Identity,
                      bias=bgate_c[:, k:k + 1], scale=1.0 / W_SCALE).then_inc(gate_ready, 1)

            s.wait_ge(y_ready, PAIRS)
            up_and_gate(0)
            with s.Fori(1, PAIRS) as i:
                up_and_gate(i)

            s.wait_ge(vswap_ready, 1)
            s.dma_start(rc[0:E, 9:10], rc[E:P, 8:9]).then_inc(vswap_in, 16)
            s.dma_start(rc[E:P, 9:10], rc[0:E, 8:9]).then_inc(vswap_in, 16)

            def fs_high(i, par):
                s.wait_ge(fsn_ready, i + 1)
                dst = fs2[:, par * PT:(par + 1) * PT]
                A(dst[0:E, 0:L], fsn[0:E, :], ACT.Copy, scale=FS_SCALE)
                A(dst[0:E, L:PT], fsn[E:P, :], ACT.Copy, scale=FS_SCALE)
                A(fs_h1[E:P, :], fsn[E:P, :], ACT.Copy, scale=FS_SCALE).then_inc(fs_hi_ready, 1)

            def high_part(g, k):
                s.wait_ge(weighted, g + 1)
                wait_pairs(s, down_done, g + 1 - RING)
                A(act_hi[:, k % RING, :], act[:, k % RING, :], ACT.Copy).then_inc(hi_ready, 1)

            def gate_experts(i, par):
                s.wait_ge(out_done, i + 1)
                wait_pairs(s, tr5_done, i)
                for h in range(2):
                    last = A(oT[:, h * L:(h + 1) * L], bank[6 + par][:, h * L:(h + 1) * L], ACT.Copy,
                             scale=mod[:, 5, bass.ds(i + h * PAIRS, 1)])
                last.then_inc(o_ready, 1)

            def store(i):
                s.wait_ge(fin_ready, i + 1)
                for h in range(2):
                    s.dma_start(out_view[bass.ds(i, 1), h].rearrange("a p s d -> (a p) s d"),
                                pair_cols(xres, i)[:, h * L:(h + 1) * L].rearrange("p (s d) -> p s d", d=D)
                                ).then_inc(stored, 16)

            def experts(i, par, first=False, last=False):
                for k in range(CH):
                    high_part(i * CH + k, k)
                    if k == 5 and not first:
                        gate_experts(i - 1, 1 - par)
                    if k == 9 and not last:
                        fs_high(i + 1, 1 - par)
                    if k == 11 and not first:
                        store(i - 1)

            fs_high(0, 0)
            run_experts(s, experts)
            gate_experts(PAIRS - 1, 1)
            store(PAIRS - 1)
            s.wait_ge(stored, 32 * PAIRS)

        @block.tensor
        def _(pe):
            M = nc.tensor.matmul
            T = nc.tensor.transpose
            pe.wait_ge(first_in, 48)
            pe.wait_ge(c_silu, 1)
            T(bank[0][:, 0:B], cs_sb[:], ident[0:B, 0:B]).then_inc(cT_done, 1)
            pe.wait_ge(cT_copied, 1)
            for m in range(6):
                last = M(bank[1][:, m * B:(m + 1) * B], sort_c[:, m * D:(m + 1) * D], cT[:], start=True, stop=True)
            last.then_inc(mod_done, 1)
            pe.wait_ge(params_in, N_PARAMS)
            M(bank[2][:, 0:1], wp_sb[:], cols[:, 0:1], start=True, stop=True).then_inc(biasp_done, 1)
            pe.wait_ge(prep_done, 1)
            pe.wait_ge(zeroed, 5)

            def turn1(i):
                pe.wait_ge(xn_ready[0], i + 1)
                wait_pairs(pe, h_ready, i)
                for t in range(TILES):
                    last = T(t1_ps[:, t * P:(t + 1) * P], xn1[:, t, :], ident)
                last.then_inc(tr1_done, 1)

            def project(i):
                pe.wait_ge(h_ready, i + 1)
                wait_pairs(pe, psum_taken, i)
                M(u_ps[0:N, :].rearrange("p (h t) -> p h t", h=2), ws_sb[:], hT[:, :, PAD:ROW], start=True, stop=True)
                for k in range(TAPS):
                    last = M(proj_ps[:].rearrange("p (h t) -> p h t", h=2), wtap[:, k, :], hT[:, :, k:k + L],
                             start=(k == 0), stop=(k == TAPS - 1))
                last.then_inc(proj_done, 1)

            def attention_out(i):
                pe.wait_ge(y_ready, i + 1)
                wait_pairs(pe, att_ready, i)
                M(o_ps[:, 0:L], wo_a[:], y[:], start=True, stop=True)
                M(o_ps[:, L:PT], wo_b[:], y[:], start=True, stop=True).then_inc(wo_done, 1)

            def turn2(i):
                pe.wait_ge(att_ready, i + 1)
                wait_pairs(pe, resid_done, i)
                for t in range(TILES):
                    last = T(t2_ps[:, t * P:(t + 1) * P], att[:, t * P:(t + 1) * P], ident)
                last.then_inc(tr2_done, 1)

            def turn3(i):
                pe.wait_ge(xn_ready[1], i + 1)
                wait_pairs(pe, h2_ready, i)
                for t in range(TILES):
                    last = T(t3_ps[:, t * P:(t + 1) * P], xn2[:, t, :], ident)
                last.then_inc(tr3_done, 1)

            def router(i):
                pe.wait_ge(h2_ready, i + 1)
                wait_pairs(pe, shifted, i)
                for h in range(2):
                    for p in range(TILES // 2):
                        t, k = h * (TILES // 2) + p, p * 2 + h
                        last = M(lg_ps[:, k * E:(k + 1) * E], h2[:, t * P:(t + 1) * P], wr_sb[:], start=True, stop=True)
                last.then_inc(router_done, 1)

            def turn4(i):
                pe.wait_ge(sc_ready, i + 1)
                wait_pairs(pe, s_ready, i)
                for p in range(TILES // 2):
                    last = T(t4_ps[:, p * P:(p + 1) * P], sc[:, 2 * p:2 * p + 2, :].rearrange("p t e -> p (t e)"), ident)
                last.then_inc(tr4_done, 1)

            run_pairs(pe, ((turn1, 1), (attention_out, 3), (turn3, 5), (project, 1), (turn2, 3), (turn4, 7), (router, 5)))

            def chunk_w(t, k):
                return t[:, k * P:(k + 1) * P]

            def three_products(dst, w_hi, w_lo, hi, lo):
                M(dst, w_hi, hi, start=True, stop=False)
                M(dst, w_hi, lo, start=False, stop=False)
                return M(dst, w_lo, hi, start=False, stop=True)

            def up_and_gate(i):
                pe.wait_ge(split_done, i + 1)
                hi, lo = pair_cols(h2_hi, i), pair_cols(h2_lo, i)
                for k in range(CH):
                    wait_pairs(pe, silu_done, i * CH + k - 3)
                    three_products(bank[k % 4][:], chunk_w(up_hi, k), chunk_w(up_lo, k), hi, lo).then_inc(up_done, 1)
                    wait_pairs(pe, gate_ready, i * CH + k - 3)
                    three_products(bank[4 + k % 4][:], chunk_w(gate_hi, k), chunk_w(gate_lo, k), hi,
                                   lo).then_inc(gate_done, 1)

            pe.wait_ge(wsplit_done, WEIGHT_PIECES)
            for read in (h_ready, psum_taken, att_ready, resid_done, h2_ready, shifted, s_ready):
                pe.wait_ge(read, PAIRS)
            up_and_gate(0)
            with pe.Fori(1, PAIRS) as i:
                up_and_gate(i)
            pe.wait_ge(silu_done, PAIRS * CH)
            pe.wait_ge(gate_ready, PAIRS * CH)

            ones = const("ones")
            with pe.Fori(0, DIGITS) as i:
                pe.wait_ge(cnt_ready, i + 1)
                M(bank[0][:, 0:DIGIT], ones, rc[:, 24:24 + DIGIT], start=True, stop=True).then_inc(cnt_summed, 1)
            pe.wait_ge(cnt_ready, DIGITS + 1)
            M(bank[0][:, 0:1], ones, rc[:, 24:25], start=True, stop=True).then_inc(cnt_summed, 1)
            pe.wait_ge(tie_ready, 1)
            M(bank[1][:, 0:NG], const("same_half"), gw[:, 2, :], start=True, stop=True)
            M(bank[2][:, 0:NG], const("before"), gw[:, 2, :], start=True, stop=True)
            M(bank[3][:, 0:1], ones, rc[:, 4:5], start=True, stop=True)
            M(bank[3][:, 1:2], const("from_half0"), rc[:, 5:6], start=True, stop=True).then_inc(tie_done, 1)
            pe.wait_ge(rsum_ready, 1)
            M(bank[4][:, 0:1], const("pair_sum"), rc[:, 13:14], start=True, stop=True).then_inc(rsum_done, 1)
            pe.wait_ge(rsum_ready, 2)
            M(bank[4][:, 2:3], const("pair_sum"), rc[:, 18:19], start=True, stop=True)
            M(bank[4][:, 3:4], const("shift_up"), rc[:, 19:20], start=True, stop=True).then_inc(rsum_done, 1)

            def denominators(i, par):
                pe.wait_ge(fsn_ready, i + 1)
                for p in range(TILES // 2):
                    last = M(bank[6 + par][:, 2 * p:2 * p + 2], fsn[:, p * P:(p + 1) * P], const("same_half")[:, 0:P:E],
                             start=True, stop=True)
                last.then_inc(den_done, 1)

            def down(i, k, par):
                g, acc, slot = i * CH + k, bank[6 + par], k % RING
                if k == 0:
                    pe.wait_ge(rden_ready, i + 1)
                    M(acc[:, 0:L], bd_a[:], fsn[:], start=True, stop=False, skip_group_check=True)
                    M(acc[:, L:PT], bd_b[:], fsn[:], start=False, stop=False, skip_group_check=True)
                wait_low(pe, i, k)
                M(acc[:], chunk_w(down_hi, k), act_hi[:, slot, :], start=False, stop=False, skip_group_check=True)
                M(acc[:], chunk_w(down_lo, k), act_hi[:, slot, :], start=False, stop=False, skip_group_check=True)
                M(acc[:], chunk_w(down_hi, k), act_lo[:, slot, :], start=False, stop=(k == CH - 1),
                  skip_group_check=True).then_inc(out_done if k == CH - 1 else down_done, 1)
                if k == CH - 1:
                    pe.wait_ge(out_done, i + 1)
                    pe.sem_inc(down_done, 1)

            def turn5(i, par):
                pe.wait_ge(o_ready, i + 1)
                for t in range(TILES):
                    last = T(bank[6 + par][:, t * P:(t + 1) * P], oT[:, t * P:(t + 1) * P], ident)
                last.then_inc(tr5_done, 1)

            LAG = 6

            def experts(i, par, first=False, last=False):
                for k in range(CH):
                    g = i * CH + k
                    if k == 0:
                        pe.wait_ge(fs2_ready, i + 1)
                    wait_pairs(pe, weighted, g - 3)
                    M(bank[k % 4][:], chunk_w(sel, k), fs2[:, par * PT:(par + 1) * PT],
                      start=True, stop=True).then_inc(fsb_done, 1)
                    if k >= LAG:
                        down(i, k - LAG, par)
                    elif not first:
                        down(i - 1, CH - LAG + k, 1 - par)
                    if k == 7 and not first:
                        turn5(i - 1, 1 - par)
                    if k == 12 and not last:
                        if not first:
                            pe.wait_ge(fin_ready, i)
                        denominators(i + 1, 1 - par)

            denominators(0, 0)
            run_experts(pe, experts)
            for k in range(CH - LAG, CH):
                down(PAIRS - 1, k, 1)
            turn5(PAIRS - 1, 1)


def shape_constants(np):
    p = np.arange(128)
    half, e = p // 64, p % 64
    src, dst = p[:, None], p[None, :]
    same = half[:, None] == half[None, :]
    blocks = [
        src == dst,
        np.ones((128, 128), bool),
        same,
        same & (src < dst),
        (half[:, None] == 0) & (half[None, :] == 1),
        dst == src + 64,
        e[:, None] == e[None, :],
        64 * half[:, None] + np.arange(64)[None, :],
    ]
    tail = np.zeros((128, 3), np.float32)
    tail[:, 0], tail[:, 1] = 1e-5, 1.0
    tail[:, 2] = 1.0 + half
    newton = np.broadcast_to(np.array([-0.5, -3.0], np.float32), (128, 2))
    digit = np.broadcast_to((np.arange(1, 8, dtype=np.int32) << 28).view(np.float32), (128, 7))
    cst = np.concatenate([np.asarray(b, np.float32) for b in blocks] + [tail, digit, newton], axis=1)
    chunk, a = np.arange(16), np.arange(128) // 32
    sel = e[:, None, None] == (4 * chunk[:, None] + a[None, :])[None]
    return cst.astype(np.float32), sel.reshape(128, 16 * 128).astype(np.float16)


def kernel(**inputs):
    import numpy as _np
    import concourse.bacc as _bacc
    from concourse import mybir as _mybir
    from concourse.bass_utils import run_bass_kernel_spmd as _run

    nc = _bacc.Bacc("TRN2", target_bir_lowering=False, num_devices=1)
    arrays, args = {}, []
    attn = {k[len("L0_attn_"):]: _np.asarray(v) for k, v in inputs.items() if k.startswith("L0_attn_")}
    ffn = {k[len("L0_ffn_"):]: _np.asarray(v) for k, v in inputs.items() if k.startswith("L0_ffn_")}
    E, D, H = ffn["Wup"].shape
    A = 128 // H

    def by_chunk(v):
        return v.reshape(E // A, A * H).T

    twice = [_np.concatenate([attn[n], attn[n]])[:, None] for n in ("bs", "A_log", "dt_log")]
    params = _np.concatenate([attn["conv_w"][:, 0].T] + [attn[n][:, None] for n in ("conv_b", "bp", "bo")] + twice
                             + [by_chunk(ffn["bup"]), by_chunk(ffn["bgate"])], axis=1)
    given = [("x", attn["x"]), ("Wp", attn["Wp"]), ("Ws", attn["Ws"]), ("Wo", attn["Wo"]), ("Wr", ffn["Wr"]),
             ("br", ffn["br"]),
             ("Wup", ffn["Wup"].transpose(1, 0, 2).reshape(D, E * H)),
             ("Wgate", ffn["Wgate"].transpose(1, 0, 2).reshape(D, E * H)),
             ("Wdown", ffn["Wdown"].reshape(E // A, A * H, D).transpose(1, 0, 2).reshape(A * H, E // A * D)),
             ("bdown", ffn["bdown"]), ("c", _np.asarray(inputs["L0_c"])), ("wmod", _np.asarray(inputs["L0_wmod"])),
             ("params", params)]
    cst, sel = shape_constants(_np)
    for name, a in given + [("consts", cst), ("selectors", sel)]:
        a = _np.ascontiguousarray(a)
        arrays[f"in_{name}"] = a
        args.append(nc.dram_tensor(f"in_{name}", a.shape, _mybir.dt.from_np(a.dtype), kind="ExternalInput").ap())
    args.append(nc.dram_tensor("out_x", (32, 256, 128), F32, kind="ExternalOutput").ap())
    adaln_kernel(nc, *args)
    r = _run(nc, [arrays], core_ids=[0])
    return r.results[0]["out_x"]
```
